# Optimizing a Trainium2 kernel written in Bass

```python
import numpy as np
import jax
import jax.numpy as jnp

def _softmax(x, axis=-1):
    return jax.nn.softmax(x, axis=axis)

def _gelu(x):
    return jax.nn.gelu(x, approximate=True)

def _silu(x):
    return jax.nn.silu(x)

def _sigmoid(x):
    return jax.nn.sigmoid(x)

def _layernorm(x, axis=-1, eps=1e-05):
    m = jnp.mean(x, axis=axis, keepdims=True)
    v = jnp.var(x, axis=axis, keepdims=True)
    return (x - m) / jnp.sqrt(v + eps)

def _scatter_add(tgt, idx, src, axis=0):
    return tgt.at[idx].add(src)

def _segment_sum(src, seg, n):
    return jax.ops.segment_sum(src, seg, n)
kernel_name = 'mk_gnn_preln_d4_gnn_r8_f9f6a8'

def setup_inputs(seed: int=0):
    np.random.seed(seed)
    _w = jnp.asarray

    def _rec_inputs():
        import jax
        import jax.numpy as jnp
        _gk = jax.random.key(seed)
        x = -0.0005121 + 1.001 * jax.random.normal(jax.random.fold_in(_gk, 1), (12500, 32), jnp.float32)
        _s = jax.random.randint(jax.random.fold_in(_gk, 2), (100000,), 0, 12500, jnp.int32)
        _d = jax.random.randint(jax.random.fold_in(_gk, 3), (100000,), 0, 12500, jnp.int32)
        _loop = jnp.arange(12500, dtype=jnp.int32)
        src = jnp.concatenate([_s, _d, _loop])
        dst = jnp.concatenate([_d, _s, _loop])
        _o = jnp.argsort(dst, stable=True)
        src = src[_o]
        dst = dst[_o]
        edge_attr3_2x32 = -8.16379e-05 + 0.999858 * jax.random.normal(jax.random.fold_in(_gk, 12), (212500, 2, 32), jnp.float32)
        edge_attr_32 = 0.000216709 + 1.00012 * jax.random.normal(jax.random.fold_in(_gk, 13), (212500, 32), jnp.float32)
        edge_attr_4 = 0.000714719 + 1.00021 * jax.random.normal(jax.random.fold_in(_gk, 14), (212500, 4), jnp.float32)
        edge_weight = 0.000452788 + 0.999756 * jax.random.normal(jax.random.fold_in(_gk, 16), (212500,), jnp.float32)
        return (x, src, dst, edge_attr3_2x32, edge_attr_32, edge_attr_4, edge_weight)
    x, src, dst, edge_attr3_2x32, edge_attr_32, edge_attr_4, edge_weight = _rec_inputs()

    def _L0_gnn_setup():
        import jax, jax.numpy as jnp
        import numpy as np
        N_NODES = 12500
        N_EDGES = 200000
        DIM1 = 32
        LEAKY_SLOPE = 0.01
        key = jax.random.key(seed)
        k1, k2, k3, k4 = jax.random.split(key, 4)
        h = jax.random.normal(k1, (N_NODES, DIM1), dtype=jnp.float32)
        attn_w = jax.random.normal(k2, (2 * DIM1,), dtype=jnp.float32) * (1.0 / np.sqrt(2 * DIM1))
        src = jax.random.randint(k3, (N_EDGES,), 0, N_NODES, dtype=jnp.int32)
        dst = jax.random.randint(k4, (N_EDGES,), 0, N_NODES, dtype=jnp.int32)
        return {'h': h, 'attn_w': attn_w, 'src': src, 'dst': dst}
    _L0_gnn_all = _L0_gnn_setup()
    _L0_gnn_in = {k: v for k, v in _L0_gnn_all.items() if k in ('attn_w',)}
    del _L0_gnn_all

    def _L1_gnn_setup():
        import jax, jax.numpy as jnp
        import numpy as np
        N_NODES = 12500
        N_EDGES = 200000
        D_FEAT = 32
        key = jax.random.key(seed)
        k1, k2, k3 = jax.random.split(key, 3)
        x = jax.random.normal(k1, (N_NODES, D_FEAT), dtype=jnp.float32)
        a = jax.random.randint(k2, (2, N_EDGES), 0, N_NODES, dtype=jnp.int64)
        e = jax.random.normal(k3, (N_EDGES,), dtype=jnp.float32)
        return {'x': x, 'a': a, 'e': e}
    _L1_gnn_all = _L1_gnn_setup()
    _L1_gnn_in = {k: v for k, v in _L1_gnn_all.items() if k in ()}
    del _L1_gnn_all

    def _L2_gnn_setup():
        import jax, jax.numpy as jnp
        import numpy as np
        N = 6250
        E = 200000
        H = 2
        F = 32
        IN = 32
        OUT = 32
        NEG_SLOPE = 0.2
        key = jax.random.key(seed)
        ks = jax.random.split(key, 11)
        s = 0.1
        return {'feat': jax.random.normal(ks[0], (N, IN), jnp.float32), 'r_feat': jax.random.normal(ks[1], (E, H, F), jnp.float32), 'src': jax.random.randint(ks[2], (E,), 0, N), 'dst': jax.random.randint(ks[3], (E,), 0, N), 'W1': jax.random.normal(ks[4], (IN, OUT), jnp.float32) * s, 'b1': jnp.zeros((OUT,), jnp.float32), 'W2s': jax.random.normal(ks[5], (IN, H * F), jnp.float32) * s, 'b2s': jnp.zeros((H * F,), jnp.float32), 'W2d': jax.random.normal(ks[6], (IN, H * F), jnp.float32) * s, 'b2d': jnp.zeros((H * F,), jnp.float32), 'attn': jax.random.normal(ks[7], (1, H, F), jnp.float32) * s}
    _L2_gnn_all = _L2_gnn_setup()
    _L2_gnn_in = {k: v for k, v in _L2_gnn_all.items() if k in ('W1', 'b1', 'W2s', 'b2s', 'W2d', 'b2d', 'attn')}
    del _L2_gnn_all

    def _L3_gnn_setup():
        import jax, jax.numpy as jnp
        import numpy as np
        MUL = 8
        N_NODES = 12500
        N_EDGES = 100000
        EDGE_DIM = 32
        MLP_DIM = 64
        W_NUMEL = 4 * MUL * MUL
        ALPHA = 0.25
        C110 = 1.0 / np.sqrt(3.0)
        SI_SCALE = 1.0 / np.sqrt(MUL)
        key = jax.random.key(seed)
        ks = jax.random.split(key, 10)
        node_attr = jax.random.normal(ks[0], (N_NODES, 4 * MUL), dtype=jnp.float32)
        edge_index = jax.random.randint(ks[1], (2, N_EDGES), 0, N_NODES, dtype=jnp.int64)
        edge_sh = jax.random.normal(ks[2], (N_EDGES, 4), dtype=jnp.float32)
        edge_feat = jax.random.normal(ks[3], (N_EDGES, EDGE_DIM), dtype=jnp.float32)
        W1 = jax.random.normal(ks[4], (EDGE_DIM, MLP_DIM), dtype=jnp.float32) / np.sqrt(EDGE_DIM)
        b1 = jnp.zeros((MLP_DIM,), dtype=jnp.float32)
        W2 = jax.random.normal(ks[5], (MLP_DIM, W_NUMEL), dtype=jnp.float32) / np.sqrt(MLP_DIM)
        b2 = jnp.zeros((W_NUMEL,), dtype=jnp.float32)
        si_w0 = jax.random.normal(ks[6], (MUL, MUL), dtype=jnp.float32)
        si_w1 = jax.random.normal(ks[7], (MUL, MUL), dtype=jnp.float32)
        return {'node_attr': node_attr, 'edge_index': edge_index, 'edge_sh': edge_sh, 'edge_feat': edge_feat, 'W1': W1, 'b1': b1, 'W2': W2, 'b2': b2, 'si_w0': si_w0, 'si_w1': si_w1}
    _L3_gnn_all = _L3_gnn_setup()
    _L3_gnn_in = {k: v for k, v in _L3_gnn_all.items() if k in ('W1', 'b1', 'W2', 'b2', 'si_w0', 'si_w1')}
    del _L3_gnn_all
    return {'x': x, 'src': src, 'dst': dst, 'edge_attr3_2x32': edge_attr3_2x32, 'edge_attr_32': edge_attr_32, 'edge_attr_4': edge_attr_4, 'edge_weight': edge_weight, 'L0_gnn_attn_w': _L0_gnn_in['attn_w'], 'L2_gnn_W1': _L2_gnn_in['W1'], 'L2_gnn_b1': _L2_gnn_in['b1'], 'L2_gnn_W2s': _L2_gnn_in['W2s'], 'L2_gnn_b2s': _L2_gnn_in['b2s'], 'L2_gnn_W2d': _L2_gnn_in['W2d'], 'L2_gnn_b2d': _L2_gnn_in['b2d'], 'L2_gnn_attn': _L2_gnn_in['attn'], 'L3_gnn_W1': _L3_gnn_in['W1'], 'L3_gnn_b1': _L3_gnn_in['b1'], 'L3_gnn_W2': _L3_gnn_in['W2'], 'L3_gnn_b2': _L3_gnn_in['b2'], 'L3_gnn_si_w0': _L3_gnn_in['si_w0'], 'L3_gnn_si_w1': _L3_gnn_in['si_w1']}

def reference(x, src, dst, edge_attr3_2x32, edge_attr_32, edge_attr_4, edge_weight, L0_gnn_attn_w, L2_gnn_W1, L2_gnn_b1, L2_gnn_W2s, L2_gnn_b2s, L2_gnn_W2d, L2_gnn_b2d, L2_gnn_attn, L3_gnn_W1, L3_gnn_b1, L3_gnn_W2, L3_gnn_b2, L3_gnn_si_w0, L3_gnn_si_w1):
    import jax
    import jax.numpy as jnp

    def _L0_gnn_ref(h, attn_w, src, dst):
        import jax, jax.numpy as jnp
        import numpy as np
        N_NODES = 12500
        N_EDGES = 200000
        DIM1 = 32
        LEAKY_SLOPE = 0.01
        N, d = h.shape
        s_src = h @ attn_w[:d]
        s_dst = h @ attn_w[d:]
        e = s_src[src] + s_dst[dst]
        e = jnp.where(e >= 0, e, LEAKY_SLOPE * e)
        m = jax.ops.segment_max(e, dst, num_segments=N)
        ex = jnp.exp(e - m[dst])
        denom = jax.ops.segment_sum(ex, dst, num_segments=N)
        alpha = ex / denom[dst]
        out = jax.ops.segment_sum(h[src] * alpha[:, None], dst, num_segments=N)
        return out

    def _L1_gnn_ref(x, a, e):
        import jax, jax.numpy as jnp
        import numpy as np
        N_NODES = 12500
        N_EDGES = 200000
        D_FEAT = 32
        src = a[0]
        tgt = a[1]
        msgs = x[src] * e[:, None]
        out = jax.ops.segment_sum(msgs, tgt, num_segments=x.shape[0])
        return out

    def _L2_gnn_ref(feat, r_feat, src, dst, W1, b1, W2s, b2s, W2d, b2d, attn):
        import jax, jax.numpy as jnp
        import numpy as np
        N = 6250
        E = 200000
        H = 2
        F = 32
        IN = 32
        OUT = 32
        NEG_SLOPE = 0.2
        n = feat.shape[0]
        feat_src = (feat @ W2s + b2s).reshape(n, H, F)
        feat_dst = (feat @ W2d + b2d).reshape(n, H, F)
        en = feat_src[src]
        ev = feat_dst[dst]
        e = jax.nn.leaky_relu(en + ev, negative_slope=NEG_SLOPE)
        e = jnp.sum(e * attn, axis=-1, keepdims=True)
        m = jax.ops.segment_max(e, dst, num_segments=n)
        m = jnp.where(jnp.isfinite(m), m, 0.0)
        ee = jnp.exp(e - m[dst])
        denom = jax.ops.segment_sum(ee, dst, num_segments=n)
        alpha = ee / jnp.maximum(denom[dst], 1e-09)
        msg = jax.nn.softmax(en * r_feat * alpha, axis=-1)
        g_agg = jax.ops.segment_sum(msg, dst, num_segments=n)
        g_sum = jnp.sum(g_agg, axis=1)
        rst = (feat + g_sum) @ W1 + b1
        return rst

    def _L3_gnn_ref(node_attr, edge_index, edge_sh, edge_feat, W1, b1, W2, b2, si_w0, si_w1):
        import jax, jax.numpy as jnp
        import numpy as np
        MUL = 8
        N_NODES = 12500
        N_EDGES = 100000
        EDGE_DIM = 32
        MLP_DIM = 64
        W_NUMEL = 4 * MUL * MUL
        ALPHA = 0.25
        C110 = 1.0 / np.sqrt(3.0)
        SI_SCALE = 1.0 / np.sqrt(MUL)
        n = node_attr.shape[0]
        e = edge_sh.shape[0]
        h = jax.nn.relu(edge_feat @ W1 + b1)
        w = (h @ W2 + b2).reshape(e, 4, MUL, MUL)
        w_000, w_011, w_101, w_110 = (w[:, 0], w[:, 1], w[:, 2], w[:, 3])
        s = node_attr[:, :MUL]
        v = node_attr[:, MUL:].reshape(n, MUL, 3)
        src, dst = (edge_index[0], edge_index[1])
        s_e = s[src]
        v_e = v[src]
        sh0 = edge_sh[:, 0]
        sh1 = edge_sh[:, 1:4]
        m0 = ALPHA * (jnp.einsum('ei,eio->eo', s_e * sh0[:, None], w_000) + C110 * jnp.einsum('eim,em,eio->eo', v_e, sh1, w_110))
        m1 = ALPHA * (jnp.einsum('ei,em,eio->eom', s_e, sh1, w_011) + jnp.einsum('eim,eio->eom', v_e * sh0[:, None, None], w_101))
        out0 = jax.ops.segment_sum(m0, dst, num_segments=n)
        out1 = jax.ops.segment_sum(m1.reshape(e, MUL * 3), dst, num_segments=n).reshape(n, MUL, 3)
        out0 = out0 + SI_SCALE * (s @ si_w0)
        out1 = out1 + SI_SCALE * jnp.einsum('nim,io->nom', v, si_w1)
        return jnp.concatenate([out0, out1.reshape(n, MUL * 3)], axis=-1)
    edge_index = jnp.stack([src, dst])
    h = jnp.maximum(_layernorm(x, axis=-1), 0.0)
    x = x + _L0_gnn_ref(h, L0_gnn_attn_w, src, dst)
    h = jnp.maximum(_layernorm(x, axis=-1), 0.0)
    x = x + _L1_gnn_ref(h, edge_index, edge_weight)
    h = jnp.maximum(_layernorm(x, axis=-1), 0.0)
    x = x + _L2_gnn_ref(h, edge_attr3_2x32, src, dst, L2_gnn_W1, L2_gnn_b1, L2_gnn_W2s, L2_gnn_b2s, L2_gnn_W2d, L2_gnn_b2d, L2_gnn_attn)
    h = jnp.maximum(_layernorm(x, axis=-1), 0.0)
    x = x + _L3_gnn_ref(h, edge_index, edge_attr_4, edge_attr_32, L3_gnn_W1, L3_gnn_b1, L3_gnn_W2, L3_gnn_b2, L3_gnn_si_w0, L3_gnn_si_w1)
    return x

_drawn_inputs = setup_inputs


def setup_inputs(seed=0):
    import zlib

    import numpy as np

    out = dict(_drawn_inputs(seed))
    spreads = {'L2_gnn_b1': (0.0, 0.3),
     'L2_gnn_b2s': (0.0, 0.8),
     'L2_gnn_b2d': (0.0, 0.8),
     'L3_gnn_b1': (0.0, 0.1),
     'L3_gnn_b2': (0.0, 0.1)}
    factors = {'edge_attr3_2x32': 8.0,
     'L0_gnn_attn_w': 5.458,
     'L2_gnn_W2s': 8.0,
     'L2_gnn_W2d': 8.0,
     'L2_gnn_attn': 8.0}
    for name, (base, spread) in spreads.items():
        noise = np.random.default_rng([zlib.crc32(name.encode()), seed]).standard_normal(out[name].shape)
        drawn = base * np.exp(spread * noise) if base else spread * noise
        out[name] = jnp.asarray(drawn.astype(out[name].dtype))
    for name, factor in factors.items():
        out[name] = (out[name] * factor).astype(out[name].dtype)
    return out
```

```python
from contextlib import ExitStack, contextmanager

import concourse.bass as bass
from concourse import mybir

F32 = mybir.dt.float32
I32 = mybir.dt.int32
BF16 = mybir.dt.bfloat16
ALU = mybir.AluOpType
ACT = mybir.ActivationFunctionType
AX = mybir.AxisListType

P = 128
N_NODES, F = 12500, 32
N_EDGES = 212500
J = -(-N_NODES // P)
NP = P * J
C = 1664
EP = P * C
T = 52
NB = C // T
NPAIR = NB // 2
RING = 16
W0 = F + 2
HF = 2 * F
MUL = 8
MM = MUL * MUL
MLP = 64
WN = 4 * MM
KB = 13
LT = 7
LSTEPS = J // LT // 2
GT = 4
NG = T // GT
ZCH = C * HF // NB
BIG = 1e38
EPS = 1e-5
TABLES_STORED = [16, 32, 64, 80]
assert EP >= N_EDGES + P and C % T == 0 and NB % RING == 0 and C % (2 * KB) == 0 and J % (2 * LT) == 0 and T % GT == 0
EDGE_PARTS = {"src": (0, 1), "dst": (1, 2), "edge_weight": (2, 3), "edge_attr4": (3, 7), "edge_attr3": (7, 7 + HF)}
EDGE_W = 7 + HF


class Steps:

    def __init__(self, engine, semaphore):
        self.engine, self.semaphore = engine, semaphore
        self.count, self.turn = 0, 0

    def then_wait(self, instruction):
        instruction.then_inc(self.semaphore, 1)
        self.count += 1
        self.engine.wait_ge(self.semaphore, self.turn + self.count)

    @contextmanager
    def loop(self, turns, per_turn):
        start = self.count
        with self.engine.Fori(0, turns) as i:
            self.turn = i * per_turn
            yield i
            assert self.count - start == per_turn, self.count - start
        self.turn, self.count = 0, start + turns * per_turn


def bc(ap, shape, axis):
    return ap.unsqueeze(axis).to_broadcast(shape)


def flat(t):
    return t[:, :, :].rearrange("p a b -> p (a b)")


def build(nc, given, out, stop=4):
    ctx = ExitStack()
    with ctx:
        ctx.enter_context(nc.allow_non_contiguous_dma(reason="one index or scalar for each row or node"))

        def sb(name, shape, dt=F32):
            return ctx.enter_context(nc.sbuf_tensor(name, shape, dt))

        def sem(name):
            return ctx.enter_context(nc.semaphore(name))

        def dram(name, shape, dt=F32):
            return nc.dram_tensor(name, shape, dt).ap()

        tab = [dram("tab0", (NP, W0)), dram("tab1", (NP, F)), dram("tab2_src", (NP, HF)), dram("tab3", (NP, F))]
        tab2_dst = dram("tab2_dst", (NP, HF))
        sums = [dram("sums0", (EP, W0)), dram("sums1", (EP, F)), dram("sums2", (EP, F)), dram("sums3", (EP, F))]
        fill0 = dram("fill0", (EP, 1))
        fill2 = dram("fill2", (EP, HF))
        logits_dram = dram("message_logits", (EP, HF))
        node_idx_dram = dram("node_idx", (3 * NP, 1), I32)
        by_rank = dram("sorted_edges", (EP, EDGE_W))
        by_rank_ef = dram("sorted_ef_t", (F, C * P))
        cursors = dram("cursors", (NP, 1), I32)
        order_dram = dram("order", (EP, 1), I32)
        by_edge = lambda ap: ap.rearrange("(p k) w -> p k w", k=C)
        by_node = lambda ap: ap.rearrange("(p j) w -> p j w", j=J)
        row = lambda ap: ap.rearrange("(o n) -> o n", o=1)

        x_sb = sb("x_sb", [P, J, F])
        h_sb = sb("h_sb", [P, J, F])
        h_flat = flat(h_sb)[:, 0:C]
        fetched = sb("fetched", [P, J * W0])
        cont = sb("cont", [P, C + 1])
        cont_big = sb("cont_big", [P, C + 1])
        iota_i = sb("iota_i", [P, P], I32)
        part_i = sb("part_i", [P, 2], I32)
        ticks = sb("ticks", [P, 2], I32)
        part_f = sb("part_f", [P, 2])
        iota_f = sb("iota_f", [P, P])
        iota_b = sb("iota_b", [P, P], BF16)
        zero_b = cont[:, 0:P // 2].bitcast(BF16)
        ident = sb("ident", [P, P])
        ones = sb("ones", [P, P])
        before = sb("before", [P, P])
        after = sb("after", [P, P])
        upto = sb("upto", [P, P])
        from_left = sb("from_left", [P, P])
        from_right = sb("from_right", [P, P])
        diag = sb("diag", [P, 4, P])
        dst_first_i = sb("dst_first_i", [P, 1], I32)
        dst_ends = sb("dst_ends", [P, 2])
        first_len = sb("first_len", [P, 2])
        first_end_i = sb("first_end_i", [P, 1], I32)
        node_idx = sb("node_idx_sb", [P, 3, J], I32)
        has_edges = sb("has_edges", [P, J])
        stat = sb("stat", [P, 4, J])
        attn_bc = sb("attn_bc", [P, 2, HF])
        row_fix = sb("row_fix", [P, HF])
        ends = sb("ends", [P, 8])
        unsorted_f = sb("unsorted_f", [P, 2])
        unsorted_i = sb("unsorted_i", [P, 1], I32)
        w_node = sb("w_node", [F + 1, P + 2 * F])
        w_mlp1 = sb("w_mlp1", [MLP, MLP + 1])
        w_mlp2 = sb("w_mlp2", [MLP + 1, WN])
        left = nc.sbuf_bytes_remaining
        arena_n = (left() if callable(left) else left) // 4 - 16
        arena = sb("arena", [P, arena_n])
        at = [0]

        def take(n, *shape, dt=F32):
            v = arena[:, at[0]:at[0] + n]
            at[0] += n
            assert at[0] <= arena_n, (at[0], arena_n)
            v = v.bitcast(dt) if dt != F32 else v
            if len(shape) == 2:
                v = v.rearrange("p (a b) -> p a b", b=shape[1])
            if len(shape) == 3:
                v = v.rearrange("p (a b c) -> p a b c", b=shape[1], c=shape[2])
            return v

        l0_table = take(J * W0, J, W0)
        at_ring = at[0]
        l0_ring = take(RING * T * W0)
        l0_rows = lambda start: l0_ring[:, bass.ds(start, T * W0)].rearrange("p (t w) -> p t w", w=W0)
        l0_zero = l0_ring[:, (RING - 1) * T * W0:(RING - 1) * T * W0 + C]
        at_sums = at[0]
        l0_sums = [take(T * W0, T, W0) for _ in range(2)]
        l0_target = take(C)
        dst_f = l0_target
        l0_idx = [take(T, dt=I32) for _ in range(2)]
        at[0] = at_sums
        dst_i = take(C, dt=I32)
        dst_lo = take(C // 2).bitcast(BF16)
        dst_hi = take(C // 2).bitcast(BF16)
        at[0] = 0
        l0_max = take(C + 1)
        l0_exp = take(2 * T, 2, T)
        l0_diff = take(2 * T, 2, T)
        l0_e = take(T)
        l0_last = take(W0)
        l0_common = take(3)
        assert at[0] <= at_ring
        onehot = [fetched[:, s * (KB * (P + J) // 2):(s + 1) * (KB * (P + J) // 2)].bitcast(BF16) for s in range(2)]
        onehot_lo = [o[:, 0:KB * P].rearrange("p (k n) -> p k n", n=P) for o in onehot]
        onehot_hi = [o[:, KB * P:KB * (P + J)].rearrange("p (k n) -> p k n", n=J) for o in onehot]
        at[0] = at_ring
        order_i = take(C, dt=I32)
        col_i = take(4, dt=I32)
        col_f = take(7)
        same = take(P)
        same_low = take(P)
        cursor_i = take(1, dt=I32)
        order_col = take(1, dt=I32)
        moved = take(EDGE_W)
        moved_ef = take(F)
        moved_ef_t = take(P)[0:F, :]
        at[0] = 0
        l1_rows = [take(T * F, T, F) for _ in range(2)]
        l1_sums = [take(T * F, T, F) for _ in range(2)]
        l1_idx = [take(T, dt=I32) for _ in range(2)]
        l1_w = [take(T) for _ in range(2)]
        l1_carry = take(F)
        l1_zero = take(ZCH)
        at[0] = 0
        lin_in = [take(LT * F, LT, F) for _ in range(2)]
        lin_t = [take(LT * P)[0:F + 1, :] for _ in range(2)]
        at_free = at[0]
        l2_logit = take(2 * C, 2, C)
        at_mid = at[0]
        l2_idx = [take(T, dt=I32) for _ in range(2)]
        l2_top = take(2 * T, T, 2)
        l2_target_carry = take(HF)
        l2_tabs = take(J * P, J, P)
        l2_rows = [take(T * HF, T, HF) for _ in range(2)]
        l2_edge = [take(T * HF, T, HF) for _ in range(2)]
        l2_target = take(T * HF, T, HF)
        at[0] = at_mid
        l2_dst_i = take(C, dt=I32)
        l2_mask = take(4 * C, 4, C)
        l2_fwd = take(2 * C, 2, C)
        l2_bwd = take(2 * C, 2, C)
        l2_m = take(2 * C, 2, C)
        l2_pick = take(P)
        at[0] = at_mid
        l2_z = [take(T * HF, T, HF) for _ in range(2)]
        l2_msg = take(T * F, T, F)
        l2_norm = take(2 * T, T, 2)
        l2_sums = [take(T * F, T, F) for _ in range(2)]
        l2_carry = take(F)
        at[0] = at_free
        l3_idx = [take(T, dt=I32) for _ in range(2)]
        l3_rows = [take(T * F, T, F) for _ in range(2)]
        l3_sh = [take(T * 4, T, 4) for _ in range(2)]
        l3_ef = [take(T * P)[0:F, :] for _ in range(2)]
        l3_h = [take(GT * P)[0:MLP + 1, :] for _ in range(2)]
        l3_p0 = take(GT * 2 * MM, GT, 2 * MM)
        l3_p1 = take(4 * GT * MM, 4, GT * MM)
        l3_scal = take(T * 2 * MUL, T, 2 * MUL)
        l3_vec = take(T * 3 * MUL, T, 3 * MUL)
        l3_dot = take(T * 3 * MUL, T, MUL, 3)
        l3_red = take(4 * T * MUL, 4, T, MUL)
        l3_msg = take(T * F, T, F)
        l3_sums = [take(T * F, T, F) for _ in range(2)]
        l3_carry = take(F)

        bank = [ctx.enter_context(nc.psum_tensor(f"bank{n}", [P, 2, 512], F32)) for n in range(4)]

        def layer_sems(n, single, double=""):
            d = {m: sem(f"l{n}_{m}") for m in ("rows_free sums_ready " + single).split()}
            return d | {m: [sem(f"l{n}_{m}{s}") for s in range(2)] for m in ("idx_loaded gathered stored " + double).split()}

        step = sem("dve_step")
        S = {n: sem(n) for n in """x_loaded dst_loaded attn_loaded w_loaded iota_made pool_tick var_ready std_ready x_ready
        x_updated x_stored table_ready zero_ready zero_stored diag_ready rows_ready onehot_made0 onehot_made1 onehot_used0
        onehot_used1 hist_done cnt_ready prefix_done node_idx_ready node_idx_stored node_idx_loaded
        order_known table_stored carry_done fix_fetched fix_ready fix_scattered nodes_fetched""".split()}
        SORT = {n: sem("sort_" + n) for n in """targets_ready row_ready cursor_fetched place_ready placed order_loaded
        column_ready moved0 moved1 moved2 ef_turned ef_ready stored dve_step tick""".split()}
        L0 = layer_sems(0, "target_scattered target_loaded first_fetched last_ready max_rows_ready diff_ready exp_done "
                           "scale_ready")
        L1 = layer_sems(1, "target_zeroed", "edge_loaded")
        L2 = layer_sems(2, "target_scattered row_fetched target_loaded target_used logits_ready dst_loaded diags_ready "
                           "rows_ready diff_ready exp_ready ends_ready others_ready alpha_ready inputs_ready ones_ready "
                           "msg_free", "edge_loaded logits_stored z_loaded scaled exp_done z_used")
        L2M = L2 | {"rows_free": L2["msg_free"]}
        L3 = layer_sems(3, "ones_ready", "edge_loaded mlp_loaded h_done h_taken w_done w_taken")
        LIN = {m: [sem(f"linear_{m}{s}") for s in range(2)] for m in "staged transposed t_ready done taken".split()}

        block = ctx.enter_context(nc.Block())

        def store_sums(engine, L, n, bufs, b, s):
            engine.wait_ge(L["sums_ready"], b + 1)
            engine.dma_start(by_edge(sums[n])[:, bass.ds(b * T, T), :], bufs[s]).then_inc(L["stored"][s], 16)

        def load_edges(engine, is_unsorted, to, name, part, done, free=None, count=0):
            with engine.If(is_unsorted == 0):
                rows = part(given[name])
                if free:
                    engine.wait_ge(free, count)
                engine.dma_start(to, rows).then_inc(done, 16)
            with engine.Else():
                a, b = EDGE_PARTS[name]
                rows = part(by_rank[:, a:b])
                if free:
                    engine.wait_ge(free, count)
                engine.dma_start(to.bitcast(F32), rows).then_inc(done, 16)

        def wait_moved(engine, columns):
            for n in range(3):
                engine.wait_ge(SORT[f"moved{n}"], columns * 32)

        def know_order(engine):
            engine.wait_ge(S["order_known"], 1)
            return engine.value_load(unsorted_i[0:1, 0:1], min_val=0, max_val=1)

        @block.sync
        def _(sp):
            sp.dma_start(dst_i, by_edge(given["dst"])[:, :, 0]).then_inc(S["dst_loaded"], 16)
            sp.dma_start(x_sb[:, :, :], by_node(given["x"])).then_inc(S["x_loaded"], 16)
            sp.dma_start(attn_bc[:, 0, :], given["attn0"].partition_broadcast(P)).then_inc(S["attn_loaded"], 16)
            sp.dma_start(attn_bc[:, 1, :], given["attn2"].partition_broadcast(P)).then_inc(S["attn_loaded"], 16)
            for to, name in ((w_node[0:F, 0:HF], "W2s"), (w_node[0:F, HF:P], "W2d"), (w_node[0:F, P:P + F], "W1"),
                             (w_node[0:F, P + F:P + 2 * F], "si"), (w_mlp1[0:F, 0:MLP], "mlp_W1"),
                             (w_mlp2[0:MLP, :], "mlp_W2")):
                sp.dma_start(to, given[name]).then_inc(S["w_loaded"], 16)
            for to, name in ((w_node[F:F + 1, 0:HF], "b2s"), (w_node[F:F + 1, HF:P], "b2d"), (w_node[F:F + 1, P:P + F], "b1"),
                             (w_mlp2[MLP:MLP + 1, :], "mlp_b2")):
                sp.dma_start(to, row(given[name])).then_inc(S["w_loaded"], 16)
            sp.dma_start(w_mlp1[0:MLP, MLP:MLP + 1], given["mlp_b1"].rearrange("(n o) -> n o", o=1))\
              .then_inc(S["w_loaded"], 16)
            sp.wait_ge(S["zero_ready"], 1)
            sp.dma_start(by_edge(fill0)[:, :, 0], l0_zero).then_inc(S["zero_stored"], 16)
            sp.wait_ge(S["table_ready"], 2)
            sp.dma_start(by_node(tab[0]), l0_table).then_inc(S["table_stored"], 16)
            is_unsorted = know_order(sp)
            with sp.If(is_unsorted != 0):
                sp.wait_ge(SORT["placed"], 32 * C)
                sp.dma_start(order_i, by_edge(order_dram)[:, :, 0]).then_inc(SORT["order_loaded"], 16)
                with sp.Fori(0, C) as k:
                    wait_moved(sp, k + 1)
                    sp.dma_start(by_edge(by_rank)[:, bass.ds(k, 1), :], moved.unsqueeze(1)).then_inc(SORT["stored"], 16)
                    sp.wait_ge(SORT["ef_ready"], k + 1)
                    sp.dma_start(by_rank_ef[:, bass.ds(k * P, P)], moved_ef_t).then_inc(SORT["stored"], 16)
                sp.wait_ge(SORT["stored"], 32 * C)

            def load_idx(L, idx, b, s, turn):
                load_edges(sp, is_unsorted, idx[s], "src", lambda ap: by_edge(ap)[:, bass.ds(b * T, T), 0],
                           L["idx_loaded"][s], L["gathered"][s], turn * (16 * T))

            with sp.Fori(0, RING // 2) as i:
                for s in range(2):
                    load_idx(L0, l0_idx, 2 * i + s, s, i)
            sp.wait_ge(S["node_idx_ready"], 1)
            load_edges(sp, is_unsorted, dst_i, "dst", lambda ap: by_edge(ap)[:, :, 0], S["dst_loaded"])
            load_edges(sp, is_unsorted, dst_first_i[:, :], "dst", lambda ap: by_edge(ap)[:, 0, :], S["dst_loaded"])
            for s in range(2):
                load_idx(L0, l0_idx, RING + s, s, RING // 2)
            sp.wait_ge(L0["target_scattered"], 16 * J)
            sp.wait_ge(S["rows_ready"], 3)
            sp.dma_start(l0_target, by_edge(fill0)[:, :, 0]).then_inc(L0["target_loaded"], 16)
            with sp.Fori(RING // 2 + 1, NPAIR) as i:
                for s in range(2):
                    load_idx(L0, l0_idx, 2 * i + s, s, i)

            def finish():
                if stop == 3:
                    for s in range(2):
                        sp.wait_ge(LIN["taken"][s], 2 * LSTEPS)
                else:
                    sp.wait_ge(S["x_updated"], min(stop, 3))
                sp.wait_ge(S["w_loaded"], 16 * 11)
                if stop > 1:
                    sp.wait_ge(L1["target_zeroed"], 16 * NB)
                sp.dma_start(by_node(out), x_sb[:, :, :]).then_inc(S["x_stored"], 16)
                sp.wait_ge(S["x_stored"], 16)

            if stop == 1:
                return finish()

            def edge_blocks(L, idx, edge, name, sums_bufs, n, more=None):
                def loads(b, s, turn):
                    load_idx(L, idx, b, s, turn)
                    load_edges(sp, is_unsorted, edge[s], name, lambda ap: by_edge(ap)[:, bass.ds(b * T, T), :],
                               L["edge_loaded"][s], L["rows_free"], b + 1)
                    if more:
                        more(b, s)

                for s in range(2):
                    loads(s, s, 0)
                with sp.Fori(1, NPAIR) as i:
                    for s in range(2):
                        loads(2 * i + s, s, i)
                        store_sums(sp, L, n, sums_bufs, 2 * i + s - 2, s)
                for s in range(2):
                    store_sums(sp, L, n, sums_bufs, NB - 2 + s, s)

            sp.wait_ge(S["x_ready"], 2)
            sp.dma_start(by_node(tab[1]), h_sb[:, :, :]).then_inc(S["table_stored"], 16)
            edge_blocks(L1, l1_idx, [w.unsqueeze(2) for w in l1_w], "edge_weight", l1_sums, 1)
            if stop == 2:
                return finish()

            for s in range(2):
                sp.wait_ge(LIN["taken"][s], LSTEPS)
            sp.dma_start(by_node(tab2_dst), l2_tabs[:, :, HF:P]).then_inc(S["table_stored"], 16)
            sp.dma_start(by_node(tab[2]), l2_tabs[:, :, 0:HF]).then_inc(S["table_stored"], 16)

            def l2_loads(b, s, turn):
                load_idx(L2, l2_idx, b, s, turn)
                load_edges(sp, is_unsorted, l2_edge[s], "edge_attr3", lambda ap: by_edge(ap)[:, bass.ds(b * T, T), :],
                           L2["edge_loaded"][s], L2["logits_stored"][s], turn * 16)

            def l2_target_load(b):
                sp.wait_ge(L2["target_used"], b)
                sp.dma_start(l2_target, by_edge(fill2)[:, bass.ds(b * T, T), :]).then_inc(L2["target_loaded"], 16)

            def l2_logits_store(b, s):
                sp.wait_ge(L2["logits_ready"], b + 1)
                sp.dma_start(by_edge(logits_dram)[:, bass.ds(b * T, T), :], l2_edge[s]).then_inc(L2["logits_stored"][s], 16)

            for s in range(2):
                l2_loads(s, s, 0)
            sp.wait_ge(L2["target_scattered"], 16 * (J + 1))
            l2_target_load(0)
            with sp.Fori(0, NPAIR - 1) as i:
                for s in range(2):
                    b = 2 * i + s
                    l2_target_load(b + 1)
                    l2_logits_store(b, s)
                    l2_loads(b + 2, s, i + 1)
            l2_target_load(NB - 1)
            for s in range(2):
                l2_logits_store(NB - 2 + s, s)
            sp.wait_ge(L2["target_used"], NB)
            for s in range(2):
                sp.wait_ge(L2["logits_stored"][s], 16 * NPAIR)
            load_edges(sp, is_unsorted, l2_dst_i, "dst", lambda ap: by_edge(ap)[:, :, 0], L2["dst_loaded"])
            sp.wait_ge(L2["alpha_ready"], 1)

            def l2_z_load(b, s, turn):
                sp.wait_ge(L2["z_used"][s], turn)
                sp.dma_start(l2_z[s], by_edge(logits_dram)[:, bass.ds(b * T, T), :]).then_inc(L2["z_loaded"][s], 16)

            for s in range(2):
                l2_z_load(s, s, 0)
            with sp.Fori(1, NPAIR) as i:
                for s in range(2):
                    l2_z_load(2 * i + s, s, i)
                    store_sums(sp, L2, 2, l2_sums, 2 * i + s - 2, s)
            for s in range(2):
                store_sums(sp, L2, 2, l2_sums, NB - 2 + s, s)
            if stop == 3:
                return finish()

            def mlp_load(b, s):
                part = lambda ap: ap[:, bass.ds(b * (T * P), T * P)]
                with sp.If(is_unsorted == 0):
                    sp.dma_start(l3_ef[s], part(given["ef_t"])).then_inc(L3["mlp_loaded"][s], 16)
                with sp.Else():
                    sp.dma_start(l3_ef[s], part(by_rank_ef)).then_inc(L3["mlp_loaded"][s], 16)

            sp.wait_ge(S["x_ready"], 4)
            sp.dma_start(by_node(tab[3]), h_sb[:, :, :]).then_inc(S["table_stored"], 16)
            edge_blocks(L3, l3_idx, l3_sh, "edge_attr4", l3_sums, 3, mlp_load)
            finish()

        @block.gpsimd
        def _(pool):
            pool.iota(iota_i[:, :], pattern=[[1, P]], base=0, channel_multiplier=0).then_inc(S["iota_made"], 1)
            pool.iota(part_i[:, 0:1], pattern=[[1, 1]], base=0, channel_multiplier=1).then_inc(S["iota_made"], 1)
            pool.iota(part_i[:, 1:2], pattern=[[1, 1]], base=0, channel_multiplier=C).then_inc(S["iota_made"], 1)
            pool.memset(ticks[:, :], 0).then_inc(S["iota_made"], 1)
            pool.wait_ge(S["iota_made"], 4)

            def gather(to, table, idx, done):
                pool.indirect_dma_start(out=to, out_offset=None, in_=table,
                                        in_offset=bass.IndirectOffsetOnAxis(ap=idx, axis=0)).then_inc(done, 16)

            def scatter(to, rows, idx, done, last):
                pool.indirect_dma_start(out=to, out_offset=bass.IndirectOffsetOnAxis(ap=idx, axis=0), in_=rows,
                                        in_offset=None, bounds_check=last, oob_is_err=False).then_inc(done, 16)

            def tick(n, count=S["pool_tick"]):
                pool.wait_ge(count, n)
                pool.tensor_tensor(ticks[:, 0:1], ticks[:, 0:1], ticks[:, 1:2], ALU.add).then_inc(count, 1)

            def finish_layer(n, L, width):
                for s in range(2):
                    pool.wait_ge(L["stored"][s], 16 * NPAIR)
                buf = row_fix[:, 0:width]
                gather(buf, sums[n], first_end_i[:, 0:1], S["fix_fetched"])
                pool.wait_ge(S["fix_ready"], n + 1)
                scatter(sums[n], buf, first_end_i[:, 0:1], S["fix_scattered"], EP - 1)
                pool.wait_ge(S["fix_scattered"], 16 * (n + 1))
                for j in range(J):
                    gather(fetched[:, j * width:(j + 1) * width], sums[n], node_idx[:, 0, j:j + 1], S["nodes_fetched"])

            def gather_blocks(n, L, rows, idx):
                with pool.Fori(0, NPAIR) as i:
                    for s in range(2):
                        pool.wait_ge(L["idx_loaded"][s], i * 16 + 16)
                        pool.wait_ge(L["rows_free"], 2 * i + s + 1)
                        tick(2 * i + s + ticked[0])
                        for t in range(T):
                            gather(rows[s][:, t, :], tab[n], idx[s][:, t:t + 1], L["gathered"][s])
                ticked[0] += NB

            is_unsorted = know_order(pool)
            with pool.If(is_unsorted != 0):
                pool.wait_ge(S["node_idx_loaded"], 16)
                pool.wait_ge(S["zero_stored"], 16)
                with pool.Fori(0, C) as k:
                    pool.wait_ge(SORT["targets_ready"], k + 1)
                    tick(2 * k, SORT["tick"])
                    gather(cursor_i, cursors, col_i[:, 0:1], SORT["cursor_fetched"])
                    pool.wait_ge(SORT["place_ready"], k + 1)
                    tick(2 * k + 1, SORT["tick"])
                    scatter(order_dram, col_i[:, 1:2], col_i[:, 2:3], SORT["placed"], EP - 1)
                    scatter(cursors, cursor_i, col_i[:, 3:4], SORT["placed"], NP - 1)
                with pool.Fori(0, C) as k:
                    pool.wait_ge(SORT["column_ready"], k + 1)
                    pool.wait_ge(SORT["stored"], k * 32)
                    tick(k + 2 * C, SORT["tick"])
                    for m, (n, (a, b)) in enumerate(EDGE_PARTS.items()):
                        gather(moved[:, a:b].bitcast(I32) if n in ("src", "dst") else moved[:, a:b], given[n], order_col,
                               SORT[f"moved{m // 2}"])
                    gather(moved_ef, given["ef"], order_col, SORT["moved2"])
                pool.wait_ge(SORT["tick"], 3 * C)
            pool.wait_ge(S["table_stored"], TABLES_STORED[0])
            pool.wait_ge(S["zero_stored"], 16)
            with pool.Fori(0, NB // RING) as i:
                for r in range(RING):
                    s, turn = r % 2, i * (RING // 2) + r // 2
                    pool.wait_ge(L0["idx_loaded"][s], turn * 16 + 16)
                    pool.wait_ge(L0["gathered"][s], turn * (16 * T))
                    pool.wait_ge(L0["rows_free"], i * RING + r + 1)
                    tick(i * RING + r)
                    for t in range(T):
                        gather(l0_ring[:, (r * T + t) * W0:(r * T + t + 1) * W0], tab[0], l0_idx[s][:, t:t + 1],
                               L0["gathered"][s])
                with pool.If(i == 0):
                    pool.wait_ge(S["node_idx_loaded"], 16)
                    for j in range(J):
                        scatter(fill0, l0_table[:, j, F + 1:F + 2], node_idx[:, 1, j:j + 1], L0["target_scattered"], EP - 1)
                    pool.wait_ge(S["dst_loaded"], 48)
                    gather(row_fix[:, 0:W0], tab[0], dst_first_i[:, 0:1], L0["first_fetched"])
            ticked = [NB]
            pool.wait_ge(L0["rows_free"], RING + NB)
            finish_layer(0, L0, W0)
            if stop == 1:
                return
            pool.wait_ge(S["table_stored"], TABLES_STORED[1])
            gather_blocks(1, L1, l1_rows, l1_idx)
            finish_layer(1, L1, F)
            if stop == 2:
                return
            for s in range(2):
                pool.wait_ge(LIN["taken"][s], LSTEPS)
            for j in range(J):
                scatter(fill2, l2_tabs[:, j, HF:P], node_idx[:, 1, j:j + 1], L2["target_scattered"], EP - 1)
            pool.wait_ge(S["table_stored"], TABLES_STORED[2])
            gather(row_fix[:, 0:HF], tab2_dst, dst_first_i[:, 0:1], L2["row_fetched"])
            pool.wait_ge(L2["row_fetched"], 16)
            pool.wait_ge(L2["target_scattered"], 16 * J)
            scatter(fill2, row_fix[:, 0:HF], part_i[:, 1:2], L2["target_scattered"], EP - 1)
            gather_blocks(2, L2, l2_rows, l2_idx)
            pool.wait_ge(L2["alpha_ready"], 1)
            with pool.Fori(0, NPAIR) as i:
                for s in range(2):
                    pool.wait_ge(L2["z_loaded"][s], i * 16 + 16)
                    tick(2 * i + s + ticked[0])
                    for h in range(2):
                        z = l2_z[s][:, :, h * F:(h + 1) * F]
                        weight = bc(l2_logit[:, h, bass.ds((2 * i + s) * T, T)], [P, T, F], 2)
                        pool.tensor_tensor(z, z, weight, ALU.mult).then_inc(L2["scaled"][s], 1)
            ticked[0] += NB
            finish_layer(2, L2, F)
            if stop == 3:
                return
            pool.wait_ge(S["table_stored"], TABLES_STORED[3])
            gather_blocks(3, L3, l3_rows, l3_idx)
            finish_layer(3, L3, F)

        @block.scalar
        def _(act):
            def std(n):
                act.wait_ge(S["var_ready"], n + 1)
                act.activation(stat[:, 2, :], stat[:, 1, :], ACT.Sqrt).then_inc(S["std_ready"], 1)

            def linear_act(turns):
                with act.Fori(0, LSTEPS) as i:
                    for s in range(2):
                        act.wait_ge(LIN["transposed"][s], i + turns)
                        act.activation(lin_in[s], h_sb[:, bass.ds((2 * i + s) * LT, LT), :], ACT.Copy)\
                           .then_inc(LIN["staged"][s], 1)
                    for s in range(2):
                        act.wait_ge(LIN["transposed"][s], i + turns + 1)
                        act.wait_ge(LIN["done"][s], i + turns)
                        act.activation(lin_t[s][0:F, :], flat(bank[s])[0:F, 0:LT * P], ACT.Copy).then_inc(LIN["t_ready"][s], 1)

            std(0)
            act.wait_ge(S["x_ready"], 1)
            act.activation(l0_table[:, :, 0:F], h_sb[:, :, :], ACT.Copy).then_inc(S["table_ready"], 1)
            is_unsorted = know_order(act)
            act.wait_ge(S["node_idx_ready"], 1)
            act.dma_start(node_idx_dram.rearrange("(c h l) o -> l c (h o)", c=3, l=P), node_idx[:, :, :])\
               .then_inc(S["node_idx_stored"], 16)
            act.dma_start(cursors.rearrange("(h l) o -> l (h o)", l=P), node_idx[:, 1, :]).then_inc(S["node_idx_stored"], 16)
            act.wait_ge(S["node_idx_stored"], 32)
            act.dma_start(node_idx[:, :, :], node_idx_dram.rearrange("(c p j) o -> p c (j o)", c=3, j=J))\
               .then_inc(S["node_idx_loaded"], 16)
            with act.If(is_unsorted != 0):
                with act.Fori(0, C) as k:
                    act.wait_ge(SORT["ef_turned"], k + 1)
                    act.wait_ge(SORT["stored"], k * 32)
                    act.activation(moved_ef_t, bank[2][0:F, 0, 0:P], ACT.Copy).then_inc(SORT["ef_ready"], 1)
            with act.Fori(0, NPAIR) as i:
                for s in range(2):
                    act.wait_ge(L0["diff_ready"], 2 * i + s + 1)
                    act.activation(l0_exp, l0_diff, ACT.Exp).then_inc(L0["exp_done"], 1)
                    store_sums(act, L0, 0, l0_sums, 2 * i + s, s)
            act.wait_ge(L0["scale_ready"], 1)
            act.activation(l0_common[:, 2:3], l0_common[:, 1:2], ACT.Exp).then_inc(L0["exp_done"], 1)
            act.wait_ge(L0["scale_ready"], 2)
            act.activation(diag[:, 3, :], diag[:, 2, :], ACT.Exp).then_inc(L0["exp_done"], 1)
            if stop == 1:
                return
            std(1)
            act.wait_ge(S["zero_ready"], 2)
            fill2_rows = fill2.rearrange("(p k) w -> p (k w)", k=C)
            with act.Fori(0, NB) as n:
                act.dma_start(fill2_rows[:, bass.ds(n * ZCH, ZCH)], l1_zero).then_inc(L1["target_zeroed"], 16)
            if stop == 2:
                return
            std(2)
            act.wait_ge(S["x_ready"], 3)
            linear_act(0)
            act.wait_ge(L2["diff_ready"], 1)
            act.activation(l2_logit, l2_m, ACT.Exp).then_inc(L2["exp_ready"], 1)
            with act.Fori(0, NPAIR) as i:
                for s in range(2):
                    act.wait_ge(L2["scaled"][s], 2 * i + 2)
                    act.activation(l2_z[s], l2_z[s], ACT.Exp).then_inc(L2["exp_done"][s], 1)
            act.wait_ge(L2["inputs_ready"], 1)
            linear_act(LSTEPS)
            if stop == 3:
                return
            std(3)
            act.wait_ge(S["x_ready"], 4)
            linear_act(2 * LSTEPS)
            with act.Fori(0, NPAIR) as i:
                for n in range(2 * NG):
                    q, turn = n % 2, i * NG + n // 2
                    act.wait_ge(L3["h_done"][q], turn + 1)
                    act.wait_ge(L3["w_done"][q], turn)
                    act.activation(l3_h[q][0:MLP, :], bank[q][0:MLP, 0, :], ACT.Relu, bias=w_mlp1[0:MLP, MLP:MLP + 1])\
                       .then_inc(L3["h_taken"][q], 1)

        @block.tensor
        def _(pe):
            pe.wait_ge(S["diag_ready"], 1)
            pe.matmul(bank[1][:, 0, 0:P], ones[:, :], diag[:, 0, :], start=True, stop=True).then_inc(S["rows_ready"], 1)
            pe.wait_ge(S["diag_ready"], 2)
            pe.matmul(bank[1][:, 1, 0:1], ones[:, :], unsorted_f[:, 0:1], start=True, stop=True).then_inc(S["rows_ready"], 1)
            pe.matmul(bank[0][:, 0, 0:J], zero_b, zero_b[:, 0:J], start=True, stop=False)
            with pe.Fori(0, C // (2 * KB)) as i:
                for s in range(2):
                    pe.wait_ge(S[f"onehot_made{s}"], i + 1)
                    for k in range(KB):
                        last = pe.matmul(bank[0][:, 0, 0:J], onehot_lo[s][:, k, :], onehot_hi[s][:, k, :],
                                         start=False, stop=False)
                    last.then_inc(S[f"onehot_used{s}"], 1)
            pe.matmul(bank[0][:, 0, 0:J], zero_b, zero_b[:, 0:J], start=False, stop=True).then_inc(S["hist_done"], 1)
            pe.wait_ge(S["cnt_ready"], 1)
            pe.matmul(bank[1][:, 0, 0:J], upto[:, :], stat[:, 0, :], start=True, stop=True)
            pe.matmul(bank[2][:, 0, 0:J], ones[:, :], stat[:, 0, :], start=True, stop=True).then_inc(S["prefix_done"], 1)
            is_unsorted = know_order(pe)
            with pe.If(is_unsorted != 0):
                with pe.Fori(0, C) as k:
                    pe.wait_ge(SORT["targets_ready"], k + 1)
                    pe.matmul(bank[2][:, 0, 0:P], ones[:, :], diag[:, 0, :], start=True, stop=True).then_inc(SORT["row_ready"], 1)
                with pe.Fori(0, C) as k:
                    pe.wait_ge(SORT["moved2"], k * 32 + 32)
                    pe.wait_ge(SORT["ef_ready"], k)
                    pe.transpose(bank[2][0:F, 0, 0:P], moved_ef, ident[:, :]).then_inc(SORT["ef_turned"], 1)
            pe.wait_ge(S["diag_ready"], 3)
            for c in range(2):
                last = pe.matmul(bank[1][:, 0, c * P:(c + 1) * P], ones[:, :], diag[:, c, :], start=True, stop=True)
            last.then_inc(S["rows_ready"], 1)
            pe.wait_ge(L0["last_ready"], 1)
            pe.matmul(bank[1][:, 0, 0:P], ones[:, :], diag[:, 0, :], start=True, stop=True).then_inc(L0["max_rows_ready"], 1)
            pe.wait_ge(L0["last_ready"], 2)
            pe.matmul(bank[2][:, 0, 0:P], ones[:, :], diag[:, 1, :], start=True, stop=True).then_inc(L0["max_rows_ready"], 1)
            pe.wait_ge(L0["last_ready"], 3)
            pe.matmul(bank[3][:, 0, 0:F + 1], diag[:, 3, :], l0_last[:, 0:F + 1], start=True, stop=True)\
              .then_inc(S["carry_done"], 1)
            if stop == 1:
                return

            def carry(L, last_sums):
                pe.wait_ge(L["rows_free"], NB + 2)
                pe.matmul(bank[3][:, 0, 0:F], from_left[:, :], last_sums, start=True, stop=True).then_inc(S["carry_done"], 1)

            def linear_pe(cols, depth, turns):
                m = cols.shape[1]
                with pe.Fori(0, LSTEPS) as i:
                    for s in range(2):
                        pe.wait_ge(LIN["staged"][s], i + turns + 1)
                        pe.wait_ge(LIN["t_ready"][s], i + turns)
                        for j in range(LT):
                            last = pe.transpose(flat(bank[s])[0:F, j * P:(j + 1) * P], lin_in[s][:, j, :], ident[:, :])
                        last.then_inc(LIN["transposed"][s], 1)
                    for s in range(2):
                        pe.wait_ge(LIN["t_ready"][s], i + turns + 1)
                        pe.wait_ge(LIN["taken"][s], i + turns)
                        for j in range(LT):
                            last = pe.matmul(flat(bank[2 + s])[:, j * m:(j + 1) * m], lin_t[s][0:depth, j * P:(j + 1) * P],
                                             cols, start=True, stop=True)
                        last.then_inc(LIN["done"][s], 1)

            carry(L1, l1_carry)
            if stop == 2:
                return
            pe.wait_ge(S["w_loaded"], 16 * 11)
            pe.wait_ge(L2["ones_ready"], 2)
            linear_pe(w_node[0:F + 1, 0:P], F + 1, 0)
            for n in range(4):
                pe.wait_ge(L2["diags_ready"], n + 1)
                pe.matmul(bank[n][:, 0, 0:P], ones[:, :], diag[:, n, :], start=True, stop=True).then_inc(L2["rows_ready"], 1)
            pe.wait_ge(L2["ends_ready"], 1)
            pe.matmul(bank[0][:, 1, 0:2], from_left[:, :], ends[:, 0:2], start=True, stop=True)
            pe.matmul(bank[1][:, 1, 0:2], from_right[:, :], ends[:, 2:4], start=True, stop=True).then_inc(L2["others_ready"], 1)
            carry(L2M, l2_carry)
            linear_pe(w_node[0:F + 1, P:P + F], F + 1, LSTEPS)
            if stop == 3:
                return
            pe.wait_ge(L3["ones_ready"], 3)
            linear_pe(w_node[0:F, P + F:P + 2 * F], F, 2 * LSTEPS)
            for s in range(2):
                pe.wait_ge(LIN["taken"][s], 3 * LSTEPS)
            with pe.Fori(0, NPAIR) as i:
                def hidden(n):
                    q, turn = n % 2, i * NG + n // 2
                    s, g = divmod(n, NG)
                    if g == 0:
                        pe.wait_ge(L3["mlp_loaded"][s], i * 16 + 16)
                    pe.wait_ge(L3["h_taken"][q], turn)
                    pe.matmul(bank[q][0:MLP, 0, :], w_mlp1[0:F, 0:MLP], l3_ef[s][:, g * GT * P:(g + 1) * GT * P],
                              start=True, stop=True).then_inc(L3["h_done"][q], 1)

                hidden(0)
                for n in range(2 * NG):
                    q, turn = n % 2, i * NG + n // 2
                    if n + 1 < 2 * NG:
                        hidden(n + 1)
                    pe.wait_ge(L3["h_taken"][q], turn + 1)
                    pe.wait_ge(L3["w_taken"][q], turn)
                    for t in range(GT):
                        last = pe.matmul(flat(bank[2 + q])[:, t * WN:(t + 1) * WN], l3_h[q][:, t * P:(t + 1) * P],
                                         w_mlp2[:, :], start=True, stop=True)
                    last.then_inc(L3["w_done"][q], 1)
            carry(L3, l3_carry)

        @block.vector
        def _(v):
            dve = Steps(v, step)
            run = dve.then_wait

            def layer_norm(n):
                sq = fetched[:, 0:J * F].rearrange("p (j f) -> p j f", f=F)
                run(v.tensor_reduce(stat[:, 0, :], x_sb[:, :, :], AX.X, ALU.add))
                run(v.tensor_scalar(stat[:, 0, :], stat[:, 0, :], 1.0 / F, None, ALU.mult))
                run(v.tensor_tensor(h_sb[:, :, :], x_sb[:, :, :], bc(stat[:, 0, :], [P, J, F], 2), ALU.subtract))
                run(v.tensor_tensor(sq, h_sb[:, :, :], h_sb[:, :, :], ALU.mult))
                run(v.tensor_reduce(stat[:, 1, :], sq, AX.X, ALU.add))
                v.tensor_scalar(stat[:, 1, :], stat[:, 1, :], 1.0 / F, EPS, ALU.mult, ALU.add).then_inc(S["var_ready"], 1)
                v.wait_ge(S["std_ready"], n + 1)
                run(v.reciprocal(stat[:, 3, :], stat[:, 2, :]))
                v.scalar_tensor_tensor(h_sb[:, :, :], h_sb[:, :, :], 0.0, bc(stat[:, 3, :], [P, J, F], 2),
                                       ALU.max, ALU.mult).then_inc(S["x_ready"], 1)
                v.wait_ge(S["x_ready"], n + 1)

            def start_blocks(L, carry):
                v.memset(carry, 0.0).then_inc(L["rows_free"], 2)

            def scan_block(L, rows, to, carry, b, turn, s):
                v.wait_ge(L["stored"][s], turn * 16)
                v.wait_ge(L["rows_free"], b + 2)
                for f in range(F):
                    ins = v.tensor_tensor_scan(to[:, :, f], cont[:, bass.ds(b * T, T)], rows[:, :, f], carry[:, f:f + 1],
                                               ALU.mult, ALU.add)
                ins.then_inc(L["sums_ready"], 1)
                v.wait_ge(L["sums_ready"], b + 1)
                v.tensor_copy(carry, to[:, T - 1, :]).then_inc(L["rows_free"], 1)

            def finish_sums(n):
                v.wait_ge(S["carry_done"], n + 1)
                v.wait_ge(S["fix_fetched"], 16 * (n + 1))
                v.tensor_tensor(row_fix[:, 0:F], row_fix[:, 0:F], bank[3][:, 0, 0:F], ALU.add).then_inc(S["fix_ready"], 1)
                v.wait_ge(S["nodes_fetched"], 16 * J * (n + 1))
                y = fetched[:, 0:J * F].rearrange("p (j f) -> p j f", f=F)
                run(v.tensor_tensor(y, y, bc(has_edges[:, :], [P, J, F], 2), ALU.mult))
                return y

            def linear_add(turns):
                with v.Fori(0, LSTEPS) as i:
                    for s in range(2):
                        v.wait_ge(LIN["done"][s], i + turns + 1)
                        got = flat(bank[2 + s])[:, 0:LT * F].rearrange("p (j f) -> p j f", f=F)
                        to = x_sb[:, bass.ds((2 * i + s) * LT, LT), :]
                        v.tensor_tensor(to, to, got, ALU.add).then_inc(LIN["taken"][s], 1)
                for s in range(2):
                    v.wait_ge(LIN["taken"][s], turns + LSTEPS)

            v.memset(l0_zero, 0.0).then_inc(S["zero_ready"], 1)
            run(v.memset(ones[:, :], 1.0))
            run(v.memset(zero_b, 0.0))
            v.wait_ge(S["iota_made"], 3)
            run(v.tensor_copy(iota_f[:, :], iota_i[:, :]))
            run(v.tensor_copy(iota_b[:, :], iota_i[:, :]))
            v.tensor_copy(part_f[:, :], part_i[:, :]).then_inc(L0["rows_free"], RING)
            v.wait_ge(L0["rows_free"], RING)
            for to, op in ((ident, ALU.is_equal), (before, ALU.is_gt), (after, ALU.is_lt), (upto, ALU.is_ge)):
                run(v.tensor_scalar(to[:, :], iota_f[:, :], part_f[:, 0:1], None, op))
            v.wait_ge(S["dst_loaded"], 16)
            run(v.tensor_copy(dst_f, dst_i))
            v.tensor_scalar(diag[:, 0, :], ident[:, :], dst_f[:, 0:1], None, ALU.mult).then_inc(S["diag_ready"], 1)
            run(v.tensor_tensor(h_flat[:, 0:C - 1], dst_f[:, 0:C - 1], dst_f[:, 1:C], ALU.is_gt))
            run(v.tensor_reduce(unsorted_f[:, 0:1], h_flat[:, 0:C - 1], AX.X, ALU.add))
            v.wait_ge(S["rows_ready"], 1)
            run(v.scalar_tensor_tensor(diag[:, 1, :], bank[1][:, 0, 0:P], dst_f[:, C - 1:C], before[:, :],
                                       ALU.is_lt, ALU.mult))
            run(v.tensor_reduce(unsorted_f[:, 1:2], diag[:, 1, :], AX.X, ALU.add))
            v.tensor_tensor(unsorted_f[:, 0:1], unsorted_f[:, 0:1], unsorted_f[:, 1:2], ALU.add).then_inc(S["diag_ready"], 1)
            v.wait_ge(S["rows_ready"], 2)
            v.tensor_scalar(unsorted_i[:, :], bank[1][:, 1, 0:1], 0.0, None, ALU.is_gt).then_inc(S["order_known"], 1)
            v.wait_ge(S["x_loaded"], 16)
            layer_norm(0)
            v.wait_ge(S["attn_loaded"], 32)
            prod = fetched[:, 0:J * F].rearrange("p (j f) -> p j f", f=F)
            run(v.tensor_tensor(prod, h_sb[:, :, :], bc(attn_bc[:, 0, 0:F], [P, J, F], 1), ALU.mult))
            run(v.tensor_reduce(l0_table[:, :, F], prod, AX.X, ALU.add))
            run(v.tensor_tensor(prod, h_sb[:, :, :], bc(attn_bc[:, 0, F:2 * F], [P, J, F], 1), ALU.mult))
            v.tensor_reduce(l0_table[:, :, F + 1], prod, AX.X, ALU.add).then_inc(S["table_ready"], 1)
            v.wait_ge(S["table_ready"], 2)
            bits = h_flat.bitcast(I32)
            run(v.tensor_scalar(bits, dst_i, P - 1, None, ALU.bitwise_and))
            v.tensor_copy(dst_lo, bits).then_inc(S["onehot_used0"], 1)
            v.wait_ge(S["onehot_used0"], 1)
            run(v.tensor_scalar(bits, dst_i, P.bit_length() - 1, None, ALU.logical_shift_right))
            v.tensor_copy(dst_hi, bits).then_inc(S["onehot_used1"], 1)
            v.wait_ge(S["onehot_used1"], 1)
            with v.Fori(0, C // (2 * KB)) as i:
                for s in range(2):
                    v.wait_ge(S[f"onehot_used{s}"], i + 1)
                    at_k = i * (2 * KB) + s * KB
                    v.tensor_tensor(onehot_lo[s], bc(dst_lo[:, bass.ds(at_k, KB)], [P, KB, P], 2),
                                    bc(iota_b[:, :], [P, KB, P], 1), ALU.is_equal)
                    v.tensor_tensor(onehot_hi[s], bc(dst_hi[:, bass.ds(at_k, KB)], [P, KB, J], 2),
                                    bc(iota_b[:, 0:J], [P, KB, J], 1), ALU.is_equal).then_inc(S[f"onehot_made{s}"], 1)
            v.wait_ge(S["hist_done"], 1)
            v.tensor_copy(stat[:, 0, :], bank[0][:, 0, 0:J]).then_inc(S["cnt_ready"], 1)
            v.wait_ge(S["prefix_done"], 1)
            v.wait_ge(S["cnt_ready"], 1)
            run(v.tensor_tensor_scan(stat[:, 1, :], ones[:, 0:J], bank[2][:, 0, 0:J], 0.0, ALU.mult, ALU.add))
            run(v.tensor_tensor(stat[:, 1, :], stat[:, 1, :], bank[2][:, 0, 0:J], ALU.subtract))
            run(v.tensor_tensor(stat[:, 1, :], stat[:, 1, :], bank[1][:, 0, 0:J], ALU.add))
            run(v.tensor_tensor(stat[:, 2, :], stat[:, 1, :], stat[:, 0, :], ALU.subtract))
            run(v.tensor_scalar(stat[:, 1, :], stat[:, 1, :], 1.0, 0.0, ALU.subtract, ALU.max))
            run(v.tensor_scalar(stat[:, 3, :], stat[:, 0, :], 0.0, float(EP), ALU.is_equal, ALU.mult))
            run(v.tensor_tensor(stat[:, 2, :], stat[:, 2, :], stat[:, 3, :], ALU.add))
            run(v.tensor_copy(node_idx[:, 0, :], stat[:, 1, :]))
            run(v.tensor_copy(node_idx[:, 1, :], stat[:, 2, :]))
            run(v.tensor_copy(node_idx[:, 2, :], stat[:, 0, :]))
            is_unsorted = know_order(v)
            v.tensor_scalar(unsorted_f[:, 1:2], unsorted_f[:, 0:1], 1.0, None, ALU.mult).then_inc(S["node_idx_ready"], 1)
            with v.If(is_unsorted != 0):
                sort = Steps(v, SORT["dve_step"])
                then = sort.then_wait
                target, rank, total, cursor, edge, last, nowhere = (col_f[:, n:n + 1] for n in range(7))
                then(v.tensor_scalar(edge, part_f[:, 1:2], 1.0, None, ALU.subtract))
                with sort.loop(C, 14) as k:
                    v.wait_ge(SORT["placed"], k * 32)
                    then(v.tensor_scalar(col_i[:, 0:1], dst_i[:, bass.ds(k, 1)], 1.0, None, ALU.mult))
                    then(v.tensor_copy(target, col_i[:, 0:1]))
                    v.tensor_scalar(diag[:, 0, :], ident[:, :], target, None, ALU.mult).then_inc(SORT["targets_ready"], 1)
                    then(v.tensor_scalar(edge, edge, 1.0, None, ALU.add))
                    then(v.tensor_copy(col_i[:, 1:2], edge))
                    v.wait_ge(SORT["row_ready"], k + 1)
                    then(v.tensor_scalar(same, bank[2][:, 0, 0:P], target, None, ALU.is_equal))
                    then(v.tensor_tensor(same_low, same, after[:, :], ALU.mult))
                    then(v.tensor_reduce(rank, same_low, AX.X, ALU.add))
                    then(v.tensor_reduce(total, same, AX.X, ALU.add))
                    then(v.tensor_scalar(last, rank, 1.0, total, ALU.add, ALU.is_equal))
                    then(v.tensor_scalar(nowhere, last, 1.0, -float(NP), ALU.subtract, ALU.mult))
                    then(v.tensor_tensor(col_i[:, 3:4], target, nowhere, ALU.add))
                    v.wait_ge(SORT["cursor_fetched"], k * 16 + 16)
                    then(v.tensor_copy(cursor, cursor_i))
                    then(v.tensor_tensor(col_i[:, 2:3], cursor, rank, ALU.add))
                    then(v.tensor_tensor(cursor, cursor, total, ALU.add))
                    v.tensor_copy(cursor_i, cursor).then_inc(SORT["place_ready"], 1)
                v.wait_ge(SORT["order_loaded"], 16)
                with v.Fori(0, C) as k:
                    wait_moved(v, k)
                    v.tensor_scalar(order_col, order_i[:, bass.ds(k, 1)], 1.0, None, ALU.mult)\
                     .then_inc(SORT["column_ready"], 1)
            v.wait_ge(S["dst_loaded"], 48)
            run(v.tensor_copy(dst_f, dst_i))
            run(v.tensor_copy(dst_ends[:, 0:1], dst_f[:, 0:1]))
            run(v.tensor_copy(dst_ends[:, 1:2], dst_f[:, C - 1:C]))
            run(v.memset(cont[:, :], 0.0))
            run(v.tensor_tensor(cont[:, 1:C], dst_f[:, 1:C], dst_f[:, 0:C - 1], ALU.is_equal))
            run(v.tensor_scalar(cont_big[:, :], cont[:, :], 1.0, BIG, ALU.subtract, ALU.mult))
            run(v.tensor_scalar(h_flat, dst_f, dst_ends[:, 0:1], None, ALU.is_equal))
            run(v.tensor_reduce(first_len[:, 0:1], h_flat, AX.X, ALU.add))
            run(v.tensor_scalar(first_len[:, 1:2], first_len[:, 0:1], part_f[:, 1:2], 1.0, ALU.add, ALU.subtract))
            run(v.tensor_copy(first_end_i[:, :], first_len[:, 1:2]))
            run(v.tensor_scalar(diag[:, 0, :], ident[:, :], dst_ends[:, 0:1], None, ALU.mult))
            v.tensor_scalar(diag[:, 1, :], ident[:, :], dst_ends[:, 1:2], None, ALU.mult).then_inc(S["diag_ready"], 1)
            v.wait_ge(S["rows_ready"], 3)
            run(v.scalar_tensor_tensor(from_left[:, :], bank[1][:, 0, 0:P], dst_ends[:, 1:2], before[:, :],
                                       ALU.is_equal, ALU.mult))
            run(v.scalar_tensor_tensor(from_right[:, :], bank[1][:, 0, P:2 * P], dst_ends[:, 0:1], after[:, :],
                                       ALU.is_equal, ALU.mult))
            v.wait_ge(S["node_idx_loaded"], 16)
            run(v.tensor_scalar(has_edges[:, :], node_idx[:, 2, :], 1.0, None, ALU.min))
            v.wait_ge(L0["target_loaded"], 16)
            v.wait_ge(L0["first_fetched"], 16)
            run(v.tensor_copy(l0_target[:, 0:1], row_fix[:, F + 1:F + 2]))
            run(v.tensor_tensor_scan(l0_target, cont[:, 0:C], l0_target, 0.0, ALU.mult, ALU.add))
            run(v.memset(l0_last, 0.0))
            run(v.memset(l0_max, 0.0))
            with dve.loop(NPAIR, 18) as i:
                for s in range(2):
                    b = i * 2 + s
                    k = b * T
                    rows = l0_rows((i % (RING // 2)) * (2 * T * W0) + s * T * W0)
                    v.wait_ge(L0["gathered"][s], i * (16 * T) + 16 * T)
                    run(v.tensor_tensor(l0_e, rows[:, :, F], l0_target[:, bass.ds(k, T)], ALU.add))
                    run(v.scalar_tensor_tensor(l0_e, l0_e, 0.01, l0_e, ALU.mult, ALU.max))
                    run(v.tensor_tensor_scan(l0_max[:, bass.ds(k + 1, T)], cont_big[:, bass.ds(k, T)], l0_e,
                                             l0_max[:, bass.ds(k, 1)], ALU.add, ALU.max))
                    run(v.tensor_tensor(l0_diff[:, 0, :], l0_max[:, bass.ds(k, T)], l0_max[:, bass.ds(k + 1, T)], ALU.subtract))
                    run(v.tensor_scalar(l0_diff[:, 0, :], l0_diff[:, 0, :], 0.0, None, ALU.min))
                    v.tensor_tensor(l0_diff[:, 1, :], l0_e, l0_max[:, bass.ds(k + 1, T)], ALU.subtract)\
                     .then_inc(L0["diff_ready"], 1)
                    v.wait_ge(L0["exp_done"], b + 1)
                    run(v.tensor_tensor(l0_exp[:, 0, :], l0_exp[:, 0, :], cont[:, bass.ds(k, T)], ALU.mult))
                    run(v.tensor_tensor(rows[:, :, 0:F], rows[:, :, 0:F], bc(l0_exp[:, 1, :], [P, T, F], 2), ALU.mult))
                    v.wait_ge(L0["stored"][s], i * 16)
                    for f in range(F + 1):
                        data = rows[:, :, f] if f < F else l0_exp[:, 1, :]
                        ins = v.tensor_tensor_scan(l0_sums[s][:, :, f], l0_exp[:, 0, :], data, l0_last[:, f:f + 1],
                                                   ALU.mult, ALU.add)
                    run(ins)
                    run(v.tensor_copy(l0_last[:, 0:F + 1], l0_sums[s][:, T - 1, 0:F + 1]))
                    v.tensor_scalar(l0_sums[s][:, :, F + 1], l0_max[:, bass.ds(k + 1, T)], 1.0, None, ALU.mult)\
                     .then_inc(L0["sums_ready"], 1)
                    v.tensor_scalar(l0_last[:, F + 1:F + 2], l0_max[:, bass.ds(k + T, 1)], 1.0, None, ALU.mult)\
                     .then_inc(L0["rows_free"], 1)
                    v.wait_ge(L0["rows_free"], b + RING + 1)
            v.tensor_scalar(diag[:, 0, :], ident[:, :], l0_last[:, F + 1:F + 2], None, ALU.mult).then_inc(L0["last_ready"], 1)
            v.wait_ge(L0["max_rows_ready"], 1)
            common, own_diff, own_weight = (l0_common[:, n:n + 1] for n in range(3))
            run(v.tensor_tensor(diag[:, 1, :], from_right[:, :], bank[1][:, 0, 0:P], ALU.mult))
            run(v.tensor_scalar(diag[:, 2, :], from_right[:, :], 1.0, BIG, ALU.subtract, ALU.mult))
            run(v.tensor_tensor(diag[:, 1, :], diag[:, 1, :], diag[:, 2, :], ALU.add))
            run(v.tensor_reduce(common, diag[:, 1, :], AX.X, ALU.max))
            v.wait_ge(S["fix_fetched"], 16)
            run(v.tensor_tensor(common, common, row_fix[:, F + 1:F + 2], ALU.max))
            v.tensor_tensor(own_diff, row_fix[:, F + 1:F + 2], common, ALU.subtract).then_inc(L0["scale_ready"], 1)
            v.tensor_scalar(diag[:, 1, :], ident[:, :], common, None, ALU.mult).then_inc(L0["last_ready"], 1)
            v.wait_ge(L0["max_rows_ready"], 2)
            run(v.tensor_scalar(diag[:, 2, :], bank[2][:, 0, 0:P], l0_last[:, F + 1:F + 2], -1.0, ALU.subtract, ALU.mult))
            v.tensor_scalar(diag[:, 2, :], diag[:, 2, :], 0.0, None, ALU.min).then_inc(L0["scale_ready"], 1)
            v.wait_ge(L0["exp_done"], NB + 2)
            v.tensor_tensor(diag[:, 3, :], diag[:, 3, :], from_left[:, :], ALU.mult).then_inc(L0["last_ready"], 1)
            v.wait_ge(S["carry_done"], 1)
            v.scalar_tensor_tensor(row_fix[:, 0:F + 1], row_fix[:, 0:F + 1], own_weight, bank[3][:, 0, 0:F + 1],
                                   ALU.mult, ALU.add).then_inc(S["fix_ready"], 1)
            v.wait_ge(S["nodes_fetched"], 16 * J)
            y = fetched[:, 0:J * W0].rearrange("p (j w) -> p j w", w=W0)
            run(v.reciprocal(stat[:, 0, :], y[:, :, F]))
            run(v.tensor_tensor(stat[:, 0, :], stat[:, 0, :], has_edges[:, :], ALU.mult))
            run(v.tensor_tensor(y[:, :, 0:F], y[:, :, 0:F], bc(stat[:, 0, :], [P, J, F], 2), ALU.mult))
            v.tensor_tensor(x_sb[:, :, :], x_sb[:, :, :], y[:, :, 0:F], ALU.add).then_inc(S["x_updated"], 1)
            v.wait_ge(S["x_updated"], 1)
            if stop == 1:
                return

            start_blocks(L1, l1_carry)
            v.memset(l1_zero, 0.0).then_inc(S["zero_ready"], 1)
            layer_norm(1)
            with dve.loop(NPAIR, 2) as i:
                for s in range(2):
                    v.wait_ge(L1["edge_loaded"][s], i * 16 + 16)
                    v.wait_ge(L1["gathered"][s], i * (16 * T) + 16 * T)
                    run(v.tensor_tensor(l1_rows[s], l1_rows[s], bc(l1_w[s], [P, T, F], 2), ALU.mult))
                    scan_block(L1, l1_rows[s], l1_sums[s], l1_carry, 2 * i + s, i, s)
            y = finish_sums(1)
            v.tensor_tensor(x_sb[:, :, :], x_sb[:, :, :], y, ALU.add).then_inc(S["x_updated"], 1)
            v.wait_ge(S["x_updated"], 2)
            if stop == 2:
                return

            v.wait_ge(L1["target_zeroed"], 16 * NB)
            for s in range(2):
                v.memset(lin_t[s][F:F + 1, :], 1.0).then_inc(L2["ones_ready"], 1)
            start_blocks(L2, l2_target_carry)
            layer_norm(2)
            with v.Fori(0, LSTEPS) as i:
                for s in range(2):
                    v.wait_ge(LIN["done"][s], i + 1)
                    got = flat(bank[2 + s])[:, 0:LT * P].rearrange("p (j f) -> p j f", f=P)
                    v.tensor_scalar(l2_tabs[:, bass.ds((2 * i + s) * LT, LT), :], got, 1.0, None, ALU.mult)\
                     .then_inc(LIN["taken"][s], 1)
            with dve.loop(NPAIR, 12) as i:
                for s in range(2):
                    b = 2 * i + s
                    rows, edge = l2_rows[s], l2_edge[s]
                    v.wait_ge(L2["target_loaded"], b * 16 + 16)
                    for f in range(HF):
                        ins = v.tensor_tensor_scan(l2_target[:, :, f], cont[:, bass.ds(b * T, T)], l2_target[:, :, f],
                                                   l2_target_carry[:, f:f + 1], ALU.mult, ALU.add)
                    run(ins)
                    run(v.tensor_copy(l2_target_carry, l2_target[:, T - 1, :]))
                    v.wait_ge(L2["edge_loaded"][s], i * 16 + 16)
                    v.wait_ge(L2["gathered"][s], i * (16 * T) + 16 * T)
                    run(v.tensor_tensor(l2_target, l2_target, rows, ALU.add))
                    v.tensor_tensor(edge, edge, rows, ALU.mult).then_inc(L2["rows_free"], 1)
                    v.wait_ge(L2["rows_free"], b + 3)
                    run(v.scalar_tensor_tensor(l2_target, l2_target, 0.2, l2_target, ALU.mult, ALU.max))
                    by_head = edge.rearrange("p t (h f) -> p t h f", h=2)
                    run(v.tensor_reduce(l2_top, by_head, AX.X, ALU.max))
                    run(v.tensor_tensor(l2_target, l2_target, bc(attn_bc[:, 1, :], [P, T, HF], 1), ALU.mult))
                    v.tensor_tensor(by_head, by_head, l2_top.unsqueeze(3).to_broadcast([P, T, 2, F]), ALU.subtract)\
                     .then_inc(L2["logits_ready"], 1)
                    v.tensor_reduce(l2_logit[:, :, bass.ds(b * T, T)].rearrange("p h t -> p t h"),
                                    l2_target.rearrange("p t (h f) -> p t h f", h=2), AX.X, ALU.add)\
                     .then_inc(L2["target_used"], 1)
                    v.wait_ge(L2["logits_ready"], b + 1)
                    v.wait_ge(L2["target_used"], b + 1)
            for s in range(2):
                v.wait_ge(L2["logits_stored"][s], 16 * NPAIR)
            for h in range(2):
                v.tensor_tensor_scan(l2_fwd[:, h, :], cont_big[:, 0:C], l2_logit[:, h, :], -BIG, ALU.add, ALU.max)
                ins = v.tensor_tensor_scan(l2_bwd[:, h, ::-1], cont_big[:, C:0:-1], l2_logit[:, h, ::-1], -BIG,
                                           ALU.add, ALU.max)
            run(ins)
            for n in range(4):
                end = l2_fwd[:, n, C - 1:C] if n < 2 else l2_bwd[:, n - 2, 0:1]
                v.tensor_scalar(diag[:, n, :], ident[:, :], end, None, ALU.mult).then_inc(L2["diags_ready"], 1)
            v.wait_ge(L2["dst_loaded"], 16)
            run(v.tensor_copy(l2_mask[:, 0, :], l2_dst_i))
            for n in range(2):
                run(v.tensor_scalar(l2_mask[:, 2 + n, :], l2_mask[:, 0, :], dst_ends[:, n:n + 1], None, ALU.is_equal))
            for n in range(2):
                ins = v.tensor_scalar(l2_mask[:, n, :], l2_mask[:, 2 + n, :], 1.0, BIG, ALU.subtract, ALU.mult)
            run(ins)
            run(v.tensor_tensor(l2_m, l2_fwd, l2_bwd, ALU.max))
            for n in range(4):
                which = from_right if n < 2 else from_left
                v.wait_ge(L2["rows_ready"], n + 1)
                run(v.tensor_scalar(l2_pick, which[:, :], 1.0, BIG, ALU.subtract, ALU.mult))
                run(v.tensor_tensor(diag[:, n, :], which[:, :], bank[n][:, 0, 0:P], ALU.mult))
                run(v.tensor_tensor(diag[:, n, :], diag[:, n, :], l2_pick, ALU.add))
                run(v.tensor_reduce(ends[:, 4 + n:5 + n], diag[:, n, :], AX.X, ALU.max))
            for n in range(4):
                h = n % 2
                run(v.scalar_tensor_tensor(l2_m[:, h, :], l2_mask[:, n // 2, :], ends[:, 4 + n:5 + n], l2_m[:, h, :],
                                           ALU.add, ALU.max))
            v.tensor_tensor(l2_m, l2_logit, l2_m, ALU.subtract).then_inc(L2["diff_ready"], 1)
            v.wait_ge(L2["exp_ready"], 1)
            for h in range(2):
                v.tensor_tensor_scan(l2_fwd[:, h, :], cont[:, 0:C], l2_logit[:, h, :], 0.0, ALU.mult, ALU.add)
                ins = v.tensor_tensor_scan(l2_bwd[:, h, ::-1], cont[:, C:0:-1], l2_logit[:, h, ::-1], 0.0, ALU.mult, ALU.add)
            run(ins)
            for n in range(4):
                end = l2_fwd[:, n, C - 1:C] if n < 2 else l2_bwd[:, n - 2, 0:1]
                ins = v.tensor_copy(ends[:, n:n + 1], end)
            ins.then_inc(L2["ends_ready"], 1)
            run(v.tensor_tensor(l2_m, l2_fwd, l2_bwd, ALU.add))
            run(v.tensor_tensor(l2_m, l2_m, l2_logit, ALU.subtract))
            v.wait_ge(L2["others_ready"], 1)
            for n in range(4):
                h = n % 2
                run(v.scalar_tensor_tensor(l2_m[:, h, :], l2_mask[:, 2 + n // 2, :], bank[n // 2][:, 1, h:h + 1],
                                           l2_m[:, h, :], ALU.mult, ALU.add))
            run(v.tensor_scalar(l2_m, l2_m, 1e-9, None, ALU.max))
            run(v.reciprocal(l2_m, l2_m))
            v.tensor_tensor(l2_logit, l2_logit, l2_m, ALU.mult).then_inc(L2["alpha_ready"], 1)
            v.wait_ge(L2["alpha_ready"], 1)
            start_blocks(L2M, l2_carry)
            with dve.loop(NPAIR, 6) as i:
                for s in range(2):
                    z = l2_z[s].rearrange("p t (h f) -> p t h f", h=2)
                    v.wait_ge(L2["exp_done"][s], i + 1)
                    run(v.tensor_reduce(l2_norm, z, AX.X, ALU.add))
                    run(v.reciprocal(l2_norm, l2_norm))
                    run(v.tensor_tensor(z, z, l2_norm.unsqueeze(3).to_broadcast([P, T, 2, F]), ALU.mult))
                    v.tensor_tensor(l2_msg, z[:, :, 0, :], z[:, :, 1, :], ALU.add).then_inc(L2["z_used"][s], 1)
                    v.wait_ge(L2["z_used"][s], i + 1)
                    scan_block(L2M, l2_msg, l2_sums[s], l2_carry, 2 * i + s, i, s)
            y = finish_sums(2)
            v.tensor_tensor(h_sb[:, :, :], h_sb[:, :, :], y, ALU.add).then_inc(L2["inputs_ready"], 1)
            linear_add(LSTEPS)
            if stop == 3:
                return

            start_blocks(L3, l3_carry)
            for q in range(2):
                v.memset(l3_h[q][MLP:MLP + 1, :], 1.0).then_inc(L3["ones_ready"], 1)
            v.wait_ge(S["w_loaded"], 16 * 11)
            v.tensor_scalar(w_node[0:F, P + F:P + 2 * F], w_node[0:F, P + F:P + 2 * F], MUL ** -0.5, None, ALU.mult)\
             .then_inc(L3["ones_ready"], 1)
            layer_norm(3)
            linear_add(2 * LSTEPS)
            with dve.loop(NPAIR, 2 * (8 + 2 * NG)) as i:
                for s in range(2):
                    rows, sh = l3_rows[s], l3_sh[s]
                    sh0 = lambda n: sh[:, :, 0:1].to_broadcast([P, T, n])
                    v.wait_ge(L3["edge_loaded"][s], i * 16 + 16)
                    v.wait_ge(L3["gathered"][s], i * (16 * T) + 16 * T)
                    run(v.tensor_scalar(sh, sh, 0.25, None, ALU.mult))
                    run(v.tensor_tensor(l3_dot, rows[:, :, MUL:F].rearrange("p t (i m) -> p t i m", m=3),
                                        bc(sh[:, :, 1:4], [P, T, MUL, 3], 2), ALU.mult))
                    run(v.tensor_tensor(l3_scal[:, :, 0:MUL], rows[:, :, 0:MUL], sh0(MUL), ALU.mult))
                    run(v.tensor_reduce(l3_scal[:, :, MUL:2 * MUL], l3_dot, AX.X, ALU.add))
                    run(v.tensor_tensor(l3_vec, rows[:, :, MUL:F], sh0(3 * MUL), ALU.mult))
                    run(v.tensor_scalar(l3_scal[:, :, MUL:2 * MUL], l3_scal[:, :, MUL:2 * MUL], 3.0 ** -0.5, None, ALU.mult))
                    for g in range(NG):
                        n = s * NG + g
                        q, turn = n % 2, i * NG + n // 2
                        cols = slice(g * GT, (g + 1) * GT)
                        w = flat(bank[2 + q]).rearrange("p (t w) -> p t w", w=WN)
                        path = lambda k: w[:, :, k * MM:(k + 1) * MM].rearrange("p t (o i) -> p t o i", i=MUL)
                        v.wait_ge(L3["w_done"][q], turn + 1)
                        v.tensor_tensor(l3_p0.rearrange("p t (o i) -> p t o i", i=2 * MUL),
                                        w[:, :, 0:2 * MM].rearrange("p t (o i) -> p t o i", i=2 * MUL),
                                        bc(l3_scal[:, cols, :], [P, GT, MUL, 2 * MUL], 2), ALU.mult)
                        v.tensor_tensor(l3_p1[:, 0, :].rearrange("p (t o i) -> p t o i", o=MUL, i=MUL), path(2),
                                        bc(rows[:, cols, 0:MUL], [P, GT, MUL, MUL], 2), ALU.mult)
                        for m in range(3):
                            ins = v.tensor_tensor(l3_p1[:, 1 + m, :].rearrange("p (t o i) -> p t o i", o=MUL, i=MUL), path(3),
                                                  bc(l3_vec[:, cols, m::3], [P, GT, MUL, MUL], 2), ALU.mult)
                        ins.then_inc(L3["w_taken"][q], 1)
                        v.wait_ge(L3["w_taken"][q], turn + 1)
                        run(v.tensor_reduce(l3_msg[:, cols, 0:MUL], l3_p0.rearrange("p t (o i) -> p t o i", i=2 * MUL),
                                            AX.X, ALU.add))
                        run(v.tensor_reduce(l3_red[:, :, cols, :].rearrange("p k t o -> p k (t o)"),
                                            l3_p1.rearrange("p k (n i) -> p k n i", i=MUL), AX.X, ALU.add))
                    vec = l3_msg[:, :, MUL:F].rearrange("p t (o m) -> p t o m", m=3)
                    for m in range(3):
                        ins = v.tensor_tensor(vec[:, :, :, m], l3_red[:, 0, :, :],
                                              sh[:, :, 1 + m:2 + m].to_broadcast([P, T, MUL]), ALU.mult)
                    run(ins)
                    for m in range(3):
                        ins = v.tensor_tensor(vec[:, :, :, m], vec[:, :, :, m], l3_red[:, 1 + m, :, :], ALU.add)
                    run(ins)
                    scan_block(L3, l3_msg, l3_sums[s], l3_carry, 2 * i + s, i, s)
            y = finish_sums(3)
            v.tensor_tensor(x_sb[:, :, :], x_sb[:, :, :], y, ALU.add).then_inc(S["x_updated"], 1)


def layout(inputs):
    import numpy as np

    def padded(name, rows, value=0):
        v = np.asarray(inputs[name])
        to = np.full((rows,) + v.shape[1:], value, v.dtype)
        to[:v.shape[0]] = v
        return to.reshape(rows, -1)

    def same(name):
        return np.ascontiguousarray(inputs[name])

    def by_output(w):
        w = w.reshape(-1, 4, MUL, MUL).transpose(0, 1, 3, 2)
        both = np.concatenate([w[:, 0], w[:, 3]], axis=2)
        return np.concatenate([v.reshape(len(w), -1) for v in (both, w[:, 1], w[:, 2])], axis=1)

    si = np.zeros((F, F), np.float32)
    si[:MUL, :MUL] = inputs["L3_gnn_si_w0"]
    for m in range(3):
        si[MUL + m::3, MUL + m::3] = inputs["L3_gnn_si_w1"]
    ef = padded("edge_attr_32", EP)
    return {
        "x": padded("x", NP),
        "src": padded("src", EP),
        "dst": padded("dst", EP, N_NODES),
        "edge_weight": padded("edge_weight", EP),
        "edge_attr4": padded("edge_attr_4", EP),
        "edge_attr3": padded("edge_attr3_2x32", EP),
        "ef": ef,
        "ef_t": np.ascontiguousarray(ef.reshape(P, C, F).transpose(2, 1, 0)).reshape(F, C * P),
        "attn0": same("L0_gnn_attn_w"),
        "attn2": same("L2_gnn_attn").reshape(HF),
        "W2s": same("L2_gnn_W2s"), "b2s": same("L2_gnn_b2s"),
        "W2d": same("L2_gnn_W2d"), "b2d": same("L2_gnn_b2d"),
        "W1": same("L2_gnn_W1"), "b1": same("L2_gnn_b1"),
        "si": si,
        "mlp_W1": same("L3_gnn_W1"), "mlp_b1": same("L3_gnn_b1"),
        "mlp_W2": np.ascontiguousarray(by_output(same("L3_gnn_W2"))),
        "mlp_b2": np.ascontiguousarray(by_output(same("L3_gnn_b2")[None])[0]),
    }


def kernel(**inputs):
    import concourse.bacc as bacc
    from concourse.bass_utils import run_bass_kernel_spmd

    arrays = layout(inputs)
    nc = bacc.Bacc("TRN2", target_bir_lowering=False, num_devices=1)
    aps = {n: nc.dram_tensor(f"in_{n}", v.shape, mybir.dt.from_np(v.dtype), kind="ExternalInput").ap()
           for n, v in arrays.items()}
    out = nc.dram_tensor("out_x", (NP, F), F32, kind="ExternalOutput").ap()
    build(nc, aps, out)
    r = run_bass_kernel_spmd(nc, [{f"in_{n}": v for n, v in arrays.items()}], core_ids=[0])
    return r.results[0]["out_x"][:N_NODES]
```

```python
from contextlib import ExitStack, contextmanager

import concourse.bass as bass
from concourse import mybir

F32 = mybir.dt.float32
I32 = mybir.dt.int32
BF16 = mybir.dt.bfloat16
ALU = mybir.AluOpType
ACT = mybir.ActivationFunctionType
AX = mybir.AxisListType

P = 128
N_NODES, F = 12500, 32
N_EDGES = 212500
J = -(-N_NODES // P)
NP = P * J
C = 1664
EP = P * C
T = 52
NB = C // T
NPAIR = NB // 2
ZRING = 4
RING = 16
AHEAD = 10
W0 = F + 2
HF = 2 * F
MUL = 8
MM = MUL * MUL
MLP = 64
WN = 4 * MM
KB = 13
LT = 7
LSTEPS = J // LT // 2
GT = 4
NG = T // GT
SCANS = 3
ZCH = C * HF // NB
TICKS = {1: NB, 2: 2 * NB, "messages": 3 * NB, 3: 4 * NB}
BIG = 1e38
EPS = 1e-5
CHUNK = 2 * LT
NORMS = [0, 1, 1 + LSTEPS, 1 + 2 * LSTEPS]
TABLES_STORED = [16, 16 * (1 + LSTEPS), 16 * (1 + 3 * LSTEPS), 16 * (1 + 4 * LSTEPS)]
assert EP >= N_EDGES + P and C % T == 0 and NB % RING == 0 and C % (2 * KB) == 0 and J % (2 * LT) == 0 and T % GT == 0
EDGE_PARTS = {"src": (0, 1), "dst": (1, 2), "edge_weight": (2, 3), "edge_attr4": (3, 7), "edge_attr3": (7, 7 + HF)}
EDGE_W = 7 + HF


class Steps:

    def __init__(self, engine, semaphore):
        self.engine, self.semaphore = engine, semaphore
        self.count, self.turn = 0, 0

    def then_wait(self, instruction):
        instruction.then_inc(self.semaphore, 1)
        self.count += 1
        self.engine.wait_ge(self.semaphore, self.turn + self.count)

    @contextmanager
    def loop(self, turns, per_turn):
        start = self.count
        with self.engine.Fori(0, turns) as i:
            self.turn = i * per_turn
            yield i
            assert self.count - start == per_turn, self.count - start
        self.turn, self.count = 0, start + turns * per_turn


def bc(ap, shape, axis):
    return ap.unsqueeze(axis).to_broadcast(shape)


def flat(t):
    return t[:, :, :].rearrange("p a b -> p (a b)")


def build(nc, given, out):
    ctx = ExitStack()
    with ctx:
        ctx.enter_context(nc.allow_non_contiguous_dma(reason="one index or scalar for each row or node"))

        def sb(name, shape, dt=F32):
            return ctx.enter_context(nc.sbuf_tensor(name, shape, dt))

        def sem(name):
            return ctx.enter_context(nc.semaphore(name))

        def dram(name, shape, dt=F32):
            return nc.dram_tensor(name, shape, dt).ap()

        tab = [dram("tab0", (NP, W0)), dram("tab1", (NP, F)), dram("tab2_src", (NP, HF)), dram("tab3", (NP, F))]
        tab2_dst = dram("tab2_dst", (NP, HF))
        sums = [dram("sums0", (EP, W0)), dram("sums1", (EP, F)), dram("sums2", (EP, F)), dram("sums3", (EP, F))]
        fill0 = dram("fill0", (EP, 1))
        fill2 = dram("fill2", (EP, HF))
        logits_dram = dram("message_logits", (EP, HF))
        node_idx_dram = dram("node_idx", (3 * NP, 1), I32)
        by_rank = dram("sorted_edges", (EP, EDGE_W))
        by_rank_ef = dram("sorted_ef_t", (F, C * P))
        cursors = dram("cursors", (NP, 1), I32)
        order_dram = dram("order", (EP, 1), I32)
        by_edge = lambda ap: ap.rearrange("(p k) w -> p k w", k=C)
        by_node = lambda ap: ap.rearrange("(p j) w -> p j w", j=J)
        row = lambda ap: ap.rearrange("(o n) -> o n", o=1)

        x_sb = sb("x_sb", [P, J, F])
        h_sb = sb("h_sb", [P, J, F])
        h_flat = flat(h_sb)[:, 0:C]
        fetched = sb("fetched", [P, J * W0])
        cont = sb("cont", [P, C + 1])
        cont_big = sb("cont_big", [P, C + 1])
        iota_i = sb("iota_i", [P, P], I32)
        part_i = sb("part_i", [P, 2], I32)
        ticks = sb("ticks", [P, 2], I32)
        part_f = sb("part_f", [P, 2])
        iota_f = sb("iota_f", [P, P])
        iota_b = sb("iota_b", [P, P], BF16)
        zero_b = cont[:, 0:P // 2].bitcast(BF16)
        ident = sb("ident", [P, P])
        ones = sb("ones", [P, P])
        before = sb("before", [P, P])
        after = sb("after", [P, P])
        upto = sb("upto", [P, P])
        from_left = sb("from_left", [P, P])
        from_right = sb("from_right", [P, P])
        diag = sb("diag", [P, 4, P])
        dst_first_i = sb("dst_first_i", [P, 1], I32)
        dst_ends = sb("dst_ends", [P, 2])
        first_len = sb("first_len", [P, 2])
        first_end_i = sb("first_end_i", [P, 1], I32)
        node_idx = sb("node_idx_sb", [P, 3, J], I32)
        has_edges = sb("has_edges", [P, J])
        stat = sb("stat", [P, 4, J])
        attn_bc = sb("attn_bc", [P, 2, HF])
        row_fix = sb("row_fix", [P, HF])
        ends = sb("ends", [P, 8])
        unsorted_f = sb("unsorted_f", [P, 2])
        unsorted_i = sb("unsorted_i", [P, 1], I32)
        w_node = sb("w_node", [F + 1, P + 2 * F])
        w_mlp1 = sb("w_mlp1", [MLP, MLP + 1])
        w_mlp2 = sb("w_mlp2", [MLP + 1, WN])
        left = nc.sbuf_bytes_remaining
        arena_n = (left() if callable(left) else left) // 4 - 16
        arena = sb("arena", [P, arena_n])
        at = [0]

        def take(n, *shape, dt=F32):
            v = arena[:, at[0]:at[0] + n]
            at[0] += n
            assert at[0] <= arena_n, (at[0], arena_n)
            v = v.bitcast(dt) if dt != F32 else v
            if len(shape) == 2:
                v = v.rearrange("p (a b) -> p a b", b=shape[1])
            if len(shape) == 3:
                v = v.rearrange("p (a b c) -> p a b c", b=shape[1], c=shape[2])
            return v

        l0_table = take(J * W0, J, W0)
        at_ring = at[0]
        l0_ring = take(RING * T * W0)
        l0_rows = lambda start: l0_ring[:, bass.ds(start, T * W0)].rearrange("p (t w) -> p t w", w=W0)
        l0_zero = l0_ring[:, (RING - 1) * T * W0:(RING - 1) * T * W0 + C]
        at_sums = at[0]
        l0_sums = [take(T * W0, T, W0) for _ in range(2)]
        l0_target = take(C)
        dst_f = l0_target
        l0_idx = [take(T, dt=I32) for _ in range(2)]
        at[0] = at_sums
        dst_i = take(C, dt=I32)
        dst_lo = take(C // 2).bitcast(BF16)
        dst_hi = take(C // 2).bitcast(BF16)
        at[0] = 0
        l0_max = take(C + 1)
        l0_exp = take(2 * T, 2, T)
        l0_diff = take(2 * T, 2, T)
        l0_e = take(T)
        l0_last = take(W0)
        l0_common = take(3)
        assert at[0] <= at_ring
        onehot = [fetched[:, s * (KB * (P + J) // 2):(s + 1) * (KB * (P + J) // 2)].bitcast(BF16) for s in range(2)]
        onehot_lo = [o[:, 0:KB * P].rearrange("p (k n) -> p k n", n=P) for o in onehot]
        onehot_hi = [o[:, KB * P:KB * (P + J)].rearrange("p (k n) -> p k n", n=J) for o in onehot]
        at[0] = at_ring
        order_i = take(C, dt=I32)
        col_i = take(4, dt=I32)
        col_f = take(7)
        same = take(P)
        same_low = take(P)
        cursor_i = take(1, dt=I32)
        order_col = take(1, dt=I32)
        moved = take(EDGE_W)
        moved_ef = take(F)
        moved_ef_t = take(P)[0:F, :]
        at[0] = 0
        l1_rows = [take(T * F, T, F) for _ in range(2)]
        l1_sums = [take(T * F, T, F) for _ in range(2)]
        l1_idx = [take(T, dt=I32) for _ in range(2)]
        l1_w = [take(T) for _ in range(2)]
        l1_carry = take(F)
        l1_zero = take(ZCH)
        at[0] = 0
        lin_in = [take(LT * F, LT, F) for _ in range(2)]
        lin_t = [take(LT * P)[0:F + 1, :] for _ in range(2)]
        at_free = at[0]
        l2_logit = take(2 * C, 2, C)
        at_mid = at[0]
        l2_idx = [take(T, dt=I32) for _ in range(2)]
        l2_top = take(2 * T, T, 2)
        l2_target_carry = take(HF)
        l2_tabs = take(J * P, J, P)
        l2_rows = [take(T * HF, T, HF) for _ in range(2)]
        l2_edge = [take(T * HF, T, HF) for _ in range(2)]
        l2_target = take(T * HF, T, HF)
        at[0] = at_mid
        l2_dst_i = take(C, dt=I32)
        l2_mask = take(4 * C, 4, C)
        l2_fwd = take(2 * C, 2, C)
        l2_bwd = take(2 * C, 2, C)
        l2_pick = take(P)
        at[0] = at_mid
        l2_z = [take(T * HF, T, HF) for _ in range(ZRING)]
        l2_msg = [take(T * F, F, T) for _ in range(2)]
        l2_scanned = [take(T * F, F, T) for _ in range(2)]
        l2_goes_on = [take(T * F, F, T) for _ in range(2)]
        l2_norm = [take(2 * T, T, 2) for _ in range(2)]
        l2_cont = take(C)
        at_sums = at[0]
        l2_sums = [take(T * F, T, F) for _ in range(2)]
        at[0] = at_sums
        l2_m = take(2 * C, 2, C)
        at[0] = 0
        l3_scal = [take(T * 2 * MUL, T, 2 * MUL) for _ in range(2)]
        assert at[0] <= at_free
        at[0] = at_free
        l3_idx = [take(T, dt=I32) for _ in range(2)]
        l3_rows = [take(T * F, T, F) for _ in range(2)]
        l3_sh = [take(T * 4, T, 4) for _ in range(2)]
        l3_ef = [take(T * P)[0:F, :] for _ in range(2)]
        l3_h = [take(GT * P)[0:MLP + 1, :] for _ in range(2)]
        l3_p0 = take(GT * 2 * MM, GT, 2 * MM)
        l3_p1 = take(4 * GT * MM, 4, GT * MM)
        l3_vec = [take(T * 3 * MUL, T, 3 * MUL) for _ in range(2)]
        l3_dot = [take(T * 3 * MUL, T, MUL, 3) for _ in range(2)]
        l3_red = take(4 * T * MUL, 4, T, MUL)
        l3_msg = [take(T * F, T, F) for _ in range(2)]
        l3_sums = [take(T * F, T, F) for _ in range(2)]
        l3_carry = take(F)

        at[0] = arena_n - 3 * CHUNK * F
        chunk_x, chunk_h, chunk_sq = (take(CHUNK * F, CHUNK, F) for _ in range(3))

        bank = [ctx.enter_context(nc.psum_tensor(f"bank{n}", [P, 2, 512], F32)) for n in range(4)]

        def layer_sems(n, single, double=""):
            d = {m: sem(f"l{n}_{m}") for m in ("rows_free sums_ready " + single).split()}
            return d | {m: [sem(f"l{n}_{m}{s}") for s in range(2)] for m in ("idx_loaded gathered stored " + double).split()}

        step = sem("dve_step")
        S = {n: sem(n) for n in """x_loaded dst_loaded attn_loaded w_loaded iota_made pool_tick var_ready std_ready x_ready
        x_updated x_stored table_ready zero_ready zero_stored diag_ready rows_ready onehot_made0 onehot_made1 onehot_used0
        onehot_used1 hist_done cnt_ready prefix_done node_idx_ready node_idx_stored node_idx_loaded
        order_known table_stored carry_done fix_fetched fix_ready fix_scattered nodes_fetched0 nodes_fetched1""".split()}
        SORT = {n: sem("sort_" + n) for n in """targets_ready row_ready cursor_fetched place_ready placed order_loaded
        column_ready moved0 moved1 moved2 ef_turned ef_ready stored dve_step tick""".split()}
        L0 = layer_sems(0, "target_scattered target_loaded first_fetched last_ready max_rows_ready diff_ready exp_done "
                           "scale_ready")
        L1 = layer_sems(1, "target_zeroed", "edge_loaded")
        L2 = layer_sems(2, "target_scattered row_fetched target_loaded target_used logits_ready dst_loaded diags_ready "
                           "rows_ready diff_ready exp_ready ends_ready others_ready alpha_ready inputs_ready ones_ready "
                           "msg_free scaled exp_done normed z_used goes_on_ready", "edge_loaded logits_stored")
        Z_LOADED = [sem(f"l2_z_loaded{r}") for r in range(ZRING)]
        L3 = layer_sems(3, "ones_ready carry_ready", "edge_loaded mlp_loaded products_ready h_done h_taken w_done w_taken")
        LIN = {m: [sem(f"linear_{m}{s}") for s in range(2)] for m in "staged transposed t_ready done taken".split()}

        block = ctx.enter_context(nc.Block())

        def store_sums(engine, L, n, bufs, b, s):
            engine.wait_ge(L["sums_ready"], b + 1)
            engine.dma_start(by_edge(sums[n])[:, bass.ds(b * T, T), :], bufs[s]).then_inc(L["stored"][s], 16)

        def z_blocks(loop, lead, early, late):
            def both(i, r, with_early=True):
                if with_early:
                    early(ZRING * i + r + lead, (r + lead) % ZRING, i + (r + lead) // ZRING)
                late(ZRING * i + r, r, i)

            last = NB // ZRING - 1
            for b in range(lead):
                early(b, b, 0)
            with loop(0, last) as i:
                for r in range(ZRING):
                    both(i, r)
            for r in range(ZRING):
                both(last, r, r + lead < ZRING)

        def load_edges(engine, is_unsorted, to, name, part, done, free=None, count=0):
            with engine.If(is_unsorted == 0):
                rows = part(given[name])
                if free:
                    engine.wait_ge(free, count)
                engine.dma_start(to, rows).then_inc(done, 16)
            with engine.Else():
                a, b = EDGE_PARTS[name]
                rows = part(by_rank[:, a:b])
                if free:
                    engine.wait_ge(free, count)
                engine.dma_start(to.bitcast(F32), rows).then_inc(done, 16)

        def wait_moved(engine, columns):
            for n in range(3):
                engine.wait_ge(SORT[f"moved{n}"], columns * 32)

        def know_order(engine):
            engine.wait_ge(S["order_known"], 1)
            return engine.value_load(unsorted_i[0:1, 0:1], min_val=0, max_val=1)

        @block.sync
        def _(sp):
            sp.dma_start(dst_i, by_edge(given["dst"])[:, :, 0]).then_inc(S["dst_loaded"], 16)
            sp.dma_start(x_sb[:, :, :], by_node(given["x"])).then_inc(S["x_loaded"], 16)
            sp.dma_start(attn_bc[:, 0, :], given["attn0"].partition_broadcast(P)).then_inc(S["attn_loaded"], 16)
            sp.dma_start(attn_bc[:, 1, :], given["attn2"].partition_broadcast(P)).then_inc(S["attn_loaded"], 16)
            for to, name in ((w_node[0:F, 0:HF], "W2s"), (w_node[0:F, HF:P], "W2d"), (w_node[0:F, P:P + F], "W1"),
                             (w_node[0:F, P + F:P + 2 * F], "si"), (w_mlp1[0:F, 0:MLP], "mlp_W1"),
                             (w_mlp2[0:MLP, :], "mlp_W2")):
                sp.dma_start(to, given[name]).then_inc(S["w_loaded"], 16)
            for to, name in ((w_node[F:F + 1, 0:HF], "b2s"), (w_node[F:F + 1, HF:P], "b2d"), (w_node[F:F + 1, P:P + F], "b1"),
                             (w_mlp2[MLP:MLP + 1, :], "mlp_b2")):
                sp.dma_start(to, row(given[name])).then_inc(S["w_loaded"], 16)
            sp.dma_start(w_mlp1[0:MLP, MLP:MLP + 1], given["mlp_b1"].rearrange("(n o) -> n o", o=1))\
              .then_inc(S["w_loaded"], 16)
            sp.wait_ge(S["zero_ready"], 1)
            sp.dma_start(by_edge(fill0)[:, :, 0], l0_zero).then_inc(S["zero_stored"], 16)
            sp.wait_ge(S["table_ready"], 2)
            sp.dma_start(by_node(tab[0]), l0_table).then_inc(S["table_stored"], 16)
            is_unsorted = know_order(sp)
            with sp.If(is_unsorted != 0):
                sp.wait_ge(SORT["placed"], 32 * C)
                sp.dma_start(order_i, by_edge(order_dram)[:, :, 0]).then_inc(SORT["order_loaded"], 16)
                with sp.Fori(0, C) as k:
                    wait_moved(sp, k + 1)
                    sp.dma_start(by_edge(by_rank)[:, bass.ds(k, 1), :], moved.unsqueeze(1)).then_inc(SORT["stored"], 16)
                    sp.wait_ge(SORT["ef_ready"], k + 1)
                    sp.dma_start(by_rank_ef[:, bass.ds(k * P, P)], moved_ef_t).then_inc(SORT["stored"], 16)
                sp.wait_ge(SORT["stored"], 32 * C)

            def load_idx(L, idx, b, s, turn):
                load_edges(sp, is_unsorted, idx[s], "src", lambda ap: by_edge(ap)[:, bass.ds(b * T, T), 0],
                           L["idx_loaded"][s], L["gathered"][s], turn * (16 * T))

            with sp.Fori(0, AHEAD // 2) as i:
                for s in range(2):
                    load_idx(L0, l0_idx, 2 * i + s, s, i)
            sp.wait_ge(S["node_idx_ready"], 1)
            load_edges(sp, is_unsorted, dst_i, "dst", lambda ap: by_edge(ap)[:, :, 0], S["dst_loaded"])
            load_edges(sp, is_unsorted, dst_first_i[:, :], "dst", lambda ap: by_edge(ap)[:, 0, :], S["dst_loaded"])
            for s in range(2):
                load_idx(L0, l0_idx, AHEAD + s, s, AHEAD // 2)
            sp.wait_ge(L0["target_scattered"], 16 * J)
            sp.wait_ge(S["rows_ready"], 3)
            sp.dma_start(l0_target, by_edge(fill0)[:, :, 0]).then_inc(L0["target_loaded"], 16)
            with sp.Fori(AHEAD // 2 + 1, NPAIR) as i:
                for s in range(2):
                    load_idx(L0, l0_idx, 2 * i + s, s, i)

            def store_table(n):
                with sp.Fori(0, LSTEPS) as i:
                    chunk = bass.ds(i * CHUNK, CHUNK)
                    sp.wait_ge(S["x_ready"], NORMS[n] + 1 + i)
                    sp.dma_start(by_node(tab[n])[:, chunk, :], h_sb[:, chunk, :]).then_inc(S["table_stored"], 16)


            def edge_blocks(L, idx, edge, name, sums_bufs, n, more=None):
                def loads(b, s, turn):
                    load_idx(L, idx, b, s, turn)
                    load_edges(sp, is_unsorted, edge[s], name, lambda ap: by_edge(ap)[:, bass.ds(b * T, T), :],
                               L["edge_loaded"][s], L["rows_free"], b + 1)
                    if more:
                        more(b, s)

                for s in range(2):
                    loads(s, s, 0)
                with sp.Fori(1, NPAIR) as i:
                    for s in range(2):
                        loads(2 * i + s, s, i)
                        store_sums(sp, L, n, sums_bufs, 2 * i + s - 2, s)
                for s in range(2):
                    store_sums(sp, L, n, sums_bufs, NB - 2 + s, s)

            store_table(1)
            edge_blocks(L1, l1_idx, [w.unsqueeze(2) for w in l1_w], "edge_weight", l1_sums, 1)

            with sp.Fori(0, LSTEPS) as i:
                chunk = bass.ds(i * CHUNK, CHUNK)
                for s in range(2):
                    sp.wait_ge(LIN["taken"][s], i + 1)
                sp.dma_start(by_node(tab[2])[:, chunk, :], l2_tabs[:, chunk, 0:HF]).then_inc(S["table_stored"], 16)
                sp.dma_start(by_node(tab2_dst)[:, chunk, :], l2_tabs[:, chunk, HF:P]).then_inc(S["table_stored"], 16)

            def l2_loads(b, s, turn):
                load_idx(L2, l2_idx, b, s, turn)
                load_edges(sp, is_unsorted, l2_edge[s], "edge_attr3", lambda ap: by_edge(ap)[:, bass.ds(b * T, T), :],
                           L2["edge_loaded"][s], L2["logits_stored"][s], turn * 16)

            def l2_target_load(b):
                sp.wait_ge(L2["target_used"], b)
                sp.dma_start(l2_target, by_edge(fill2)[:, bass.ds(b * T, T), :]).then_inc(L2["target_loaded"], 16)

            def l2_logits_store(b, s):
                sp.wait_ge(L2["logits_ready"], b + 1)
                sp.dma_start(by_edge(logits_dram)[:, bass.ds(b * T, T), :], l2_edge[s]).then_inc(L2["logits_stored"][s], 16)

            for s in range(2):
                l2_loads(s, s, 0)
            sp.wait_ge(L2["target_scattered"], 16 * (J + 1))
            l2_target_load(0)
            with sp.Fori(0, NPAIR - 1) as i:
                for s in range(2):
                    b = 2 * i + s
                    l2_target_load(b + 1)
                    l2_logits_store(b, s)
                    l2_loads(b + 2, s, i + 1)
            l2_target_load(NB - 1)
            for s in range(2):
                l2_logits_store(NB - 2 + s, s)
            sp.wait_ge(L2["target_used"], NB)
            for s in range(2):
                sp.wait_ge(L2["logits_stored"][s], 16 * NPAIR)
            load_edges(sp, is_unsorted, l2_dst_i, "dst", lambda ap: by_edge(ap)[:, :, 0], L2["dst_loaded"])
            sp.wait_ge(L2["alpha_ready"], 1)

            def z_load(i, r):
                sp.dma_start(l2_z[r], by_edge(logits_dram)[:, bass.ds((ZRING * i + r) * T, T), :]).then_inc(Z_LOADED[r], 16)

            for r in range(ZRING):
                z_load(0, r)
            with sp.Fori(1, NB // ZRING) as i:
                for r in range(ZRING):
                    b = ZRING * i + r - ZRING
                    sp.wait_ge(L2["z_used"], b + 1)
                    z_load(i, r)
                    store_sums(sp, L2, 2, l2_sums, b, r % 2)
            for b in range(NB - ZRING, NB):
                store_sums(sp, L2, 2, l2_sums, b, b % 2)

            def mlp_load(b, s):
                part = lambda ap: ap[:, bass.ds(b * (T * P), T * P)]
                with sp.If(is_unsorted == 0):
                    sp.dma_start(l3_ef[s], part(given["ef_t"])).then_inc(L3["mlp_loaded"][s], 16)
                with sp.Else():
                    sp.dma_start(l3_ef[s], part(by_rank_ef)).then_inc(L3["mlp_loaded"][s], 16)

            store_table(3)
            edge_blocks(L3, l3_idx, l3_sh, "edge_attr4", l3_sums, 3, mlp_load)
            sp.wait_ge(S["w_loaded"], 16 * 11)
            sp.wait_ge(L1["target_zeroed"], 16 * NB)
            with sp.Fori(0, LSTEPS) as i:
                chunk = bass.ds(i * CHUNK, CHUNK)
                sp.wait_ge(S["x_updated"], 3 * LSTEPS + 1 + i)
                sp.dma_start(by_node(out)[:, chunk, :], x_sb[:, chunk, :]).then_inc(S["x_stored"], 16)
            sp.wait_ge(S["x_stored"], 16 * LSTEPS)

        @block.gpsimd
        def _(pool):
            pool.iota(iota_i[:, :], pattern=[[1, P]], base=0, channel_multiplier=0).then_inc(S["iota_made"], 1)
            pool.iota(part_i[:, 0:1], pattern=[[1, 1]], base=0, channel_multiplier=1).then_inc(S["iota_made"], 1)
            pool.iota(part_i[:, 1:2], pattern=[[1, 1]], base=0, channel_multiplier=C).then_inc(S["iota_made"], 1)
            pool.memset(ticks[:, :], 0).then_inc(S["iota_made"], 1)
            pool.wait_ge(S["iota_made"], 4)

            def gather(to, table, idx, done):
                pool.indirect_dma_start(out=to, out_offset=None, in_=table,
                                        in_offset=bass.IndirectOffsetOnAxis(ap=idx, axis=0)).then_inc(done, 16)

            def scatter(to, rows, idx, done, last):
                pool.indirect_dma_start(out=to, out_offset=bass.IndirectOffsetOnAxis(ap=idx, axis=0), in_=rows,
                                        in_offset=None, bounds_check=last, oob_is_err=False).then_inc(done, 16)

            def tick(n, count=S["pool_tick"]):
                pool.wait_ge(count, n)
                pool.tensor_tensor(ticks[:, 0:1], ticks[:, 0:1], ticks[:, 1:2], ALU.add).then_inc(count, 1)

            def finish_layer(n, L, width):
                for s in range(2):
                    pool.wait_ge(L["stored"][s], 16 * NPAIR)
                buf = row_fix[:, 0:width]
                gather(buf, sums[n], first_end_i[:, 0:1], S["fix_fetched"])
                pool.wait_ge(S["fix_ready"], n + 1)
                scatter(sums[n], buf, first_end_i[:, 0:1], S["fix_scattered"], EP - 1)
                pool.wait_ge(S["fix_scattered"], 16 * (n + 1))
                for j in range(J):
                    i, s = j // CHUNK, j // LT % 2
                    if i and j % LT == 0:
                        pool.wait_ge(S[f"nodes_fetched{s}"], 16 * LT * (n * LSTEPS + i))
                    gather(fetched[:, j * width:(j + 1) * width], sums[n], node_idx[:, 0, j:j + 1], S[f"nodes_fetched{s}"])

            def gather_block(n, L, rows, idx, i, s):
                pool.wait_ge(L["idx_loaded"][s], i * 16 + 16)
                pool.wait_ge(L["rows_free"], 2 * i + s + 1)
                tick(2 * i + s + TICKS[n])
                for t in range(T):
                    gather(rows[s][:, t, :], tab[n], idx[s][:, t:t + 1], L["gathered"][s])

            def gather_blocks(n, L, rows, idx):
                with pool.Fori(0, NPAIR) as i:
                    for s in range(2):
                        gather_block(n, L, rows, idx, i, s)

            is_unsorted = know_order(pool)
            with pool.If(is_unsorted != 0):
                pool.wait_ge(S["node_idx_loaded"], 16)
                pool.wait_ge(S["zero_stored"], 16)
                with pool.Fori(0, C) as k:
                    pool.wait_ge(SORT["targets_ready"], k + 1)
                    tick(2 * k, SORT["tick"])
                    gather(cursor_i, cursors, col_i[:, 0:1], SORT["cursor_fetched"])
                    pool.wait_ge(SORT["place_ready"], k + 1)
                    tick(2 * k + 1, SORT["tick"])
                    scatter(order_dram, col_i[:, 1:2], col_i[:, 2:3], SORT["placed"], EP - 1)
                    scatter(cursors, cursor_i, col_i[:, 3:4], SORT["placed"], NP - 1)
                with pool.Fori(0, C) as k:
                    pool.wait_ge(SORT["column_ready"], k + 1)
                    pool.wait_ge(SORT["stored"], k * 32)
                    tick(k + 2 * C, SORT["tick"])
                    for m, (n, (a, b)) in enumerate(EDGE_PARTS.items()):
                        gather(moved[:, a:b].bitcast(I32) if n in ("src", "dst") else moved[:, a:b], given[n], order_col,
                               SORT[f"moved{m // 2}"])
                    gather(moved_ef, given["ef"], order_col, SORT["moved2"])
                pool.wait_ge(SORT["tick"], 3 * C)
            pool.wait_ge(S["table_stored"], TABLES_STORED[0])
            pool.wait_ge(S["zero_stored"], 16)
            with pool.Fori(0, NB // RING) as i:
                for r in range(RING):
                    s, turn = r % 2, i * (RING // 2) + r // 2
                    pool.wait_ge(L0["idx_loaded"][s], turn * 16 + 16)
                    pool.wait_ge(L0["gathered"][s], turn * (16 * T))
                    pool.wait_ge(L0["rows_free"], i * RING + r + 1)
                    tick(i * RING + r)
                    for t in range(T):
                        gather(l0_ring[:, (r * T + t) * W0:(r * T + t + 1) * W0], tab[0], l0_idx[s][:, t:t + 1],
                               L0["gathered"][s])
                    if r == AHEAD - 1:
                        with pool.If(i == 0):
                            pool.wait_ge(S["node_idx_loaded"], 16)
                            for j in range(J):
                                scatter(fill0, l0_table[:, j, F + 1:F + 2], node_idx[:, 1, j:j + 1],
                                        L0["target_scattered"], EP - 1)
                            pool.wait_ge(S["dst_loaded"], 48)
                            gather(row_fix[:, 0:W0], tab[0], dst_first_i[:, 0:1], L0["first_fetched"])
            pool.wait_ge(L0["rows_free"], RING + NB)
            finish_layer(0, L0, W0)
            pool.wait_ge(S["table_stored"], TABLES_STORED[1])
            gather_blocks(1, L1, l1_rows, l1_idx)
            finish_layer(1, L1, F)
            for j in range(J):
                if j % LT == 0:
                    pool.wait_ge(LIN["taken"][j // LT % 2], j // CHUNK + 1)
                scatter(fill2, l2_tabs[:, j, HF:P], node_idx[:, 1, j:j + 1], L2["target_scattered"], EP - 1)
            pool.wait_ge(S["table_stored"], TABLES_STORED[2])
            gather(row_fix[:, 0:HF], tab2_dst, dst_first_i[:, 0:1], L2["row_fetched"])
            pool.wait_ge(L2["row_fetched"], 16)
            pool.wait_ge(L2["target_scattered"], 16 * J)
            scatter(fill2, row_fix[:, 0:HF], part_i[:, 1:2], L2["target_scattered"], EP - 1)
            gather_blocks(2, L2, l2_rows, l2_idx)
            def scale_logits(b, r, i):
                pool.wait_ge(Z_LOADED[r], i * 16 + 16)
                pool.wait_ge(L2["alpha_ready"], i + 2)
                tick(b + TICKS["messages"])
                for h in range(2):
                    z = l2_z[r][:, :, h * F:(h + 1) * F]
                    weight = bc(l2_logit[:, h, bass.ds(b * T, T)], [P, T, F], 2)
                    pool.tensor_tensor(z, z, weight, ALU.mult).then_inc(L2["scaled"], 1)

            def add_heads(b, r, i):
                pool.wait_ge(L2["normed"], b + 1)
                pool.wait_ge(L2["msg_free"], b + 1)
                pool.tensor_tensor(l2_msg[r % 2].rearrange("p f t -> p t f"), l2_z[r][:, :, 0:F], l2_z[r][:, :, F:HF],
                                   ALU.add).then_inc(L2["z_used"], 1)

            z_blocks(pool.Fori, 2, scale_logits, add_heads)
            finish_layer(2, L2, F)
            pool.wait_ge(S["table_stored"], TABLES_STORED[3])

            def products(i, s):
                rows, sh = l3_rows[s], l3_sh[s]
                sh0 = lambda n: sh[:, :, 0:1].to_broadcast([P, T, n])
                pool.wait_ge(L3["edge_loaded"][s], i * 16 + 16)
                pool.wait_ge(L3["gathered"][s], i * (16 * T) + 16 * T)
                for k in range(2):
                    pool.wait_ge(LIN["taken"][k], 3 * LSTEPS)
                pool.tensor_tensor(l3_dot[s], rows[:, :, MUL:F].rearrange("p t (i m) -> p t i m", m=3),
                                   bc(sh[:, :, 1:4], [P, T, MUL, 3], 2), ALU.mult)
                pool.tensor_tensor(l3_scal[s][:, :, 0:MUL], rows[:, :, 0:MUL], sh0(MUL), ALU.mult)
                pool.tensor_tensor(l3_vec[s], rows[:, :, MUL:F], sh0(3 * MUL), ALU.mult).then_inc(L3["products_ready"][s], 1)

            with pool.Fori(0, NPAIR) as i:
                for s in range(2):
                    gather_block(3, L3, l3_rows, l3_idx, i, s)
                    products(i, s)
            finish_layer(3, L3, F)

        @block.scalar
        def _(act):
            def std(n, i=0, count=CHUNK):
                act.wait_ge(S["var_ready"], NORMS[n] + 1 + i)
                act.activation(stat[:, 2, 0:count], stat[:, 1, 0:count], ACT.Sqrt).then_inc(S["std_ready"], 1)

            def linear_act(turns, first=lambda i: None, then=lambda i: None):
                with act.Fori(0, LSTEPS) as i:
                    first(i)
                    for s in range(2):
                        act.wait_ge(LIN["transposed"][s], i + turns)
                        act.activation(lin_in[s], h_sb[:, bass.ds((2 * i + s) * LT, LT), :], ACT.Copy)\
                           .then_inc(LIN["staged"][s], 1)
                    for s in range(2):
                        act.wait_ge(LIN["transposed"][s], i + turns + 1)
                        act.wait_ge(LIN["done"][s], i + turns)
                        act.activation(lin_t[s][0:F, :], flat(bank[s])[0:F, 0:LT * P], ACT.Copy).then_inc(LIN["t_ready"][s], 1)
                    then(i)

            std(0, 0, J)
            act.wait_ge(S["x_ready"], 1)
            act.activation(l0_table[:, :, 0:F], h_sb[:, :, :], ACT.Copy).then_inc(S["table_ready"], 1)
            is_unsorted = know_order(act)
            act.wait_ge(S["node_idx_ready"], 1)
            act.dma_start(node_idx_dram.rearrange("(c h l) o -> l c (h o)", c=3, l=P), node_idx[:, :, :])\
               .then_inc(S["node_idx_stored"], 16)
            act.dma_start(cursors.rearrange("(h l) o -> l (h o)", l=P), node_idx[:, 1, :]).then_inc(S["node_idx_stored"], 16)
            act.wait_ge(S["node_idx_stored"], 32)
            act.dma_start(node_idx[:, :, :], node_idx_dram.rearrange("(c p j) o -> p c (j o)", c=3, j=J))\
               .then_inc(S["node_idx_loaded"], 16)
            with act.If(is_unsorted != 0):
                with act.Fori(0, C) as k:
                    act.wait_ge(SORT["ef_turned"], k + 1)
                    act.wait_ge(SORT["stored"], k * 32)
                    act.activation(moved_ef_t, bank[2][0:F, 0, 0:P], ACT.Copy).then_inc(SORT["ef_ready"], 1)
            with act.Fori(0, NPAIR) as i:
                for s in range(2):
                    act.wait_ge(L0["diff_ready"], 2 * i + s + 1)
                    act.activation(l0_exp, l0_diff, ACT.Exp).then_inc(L0["exp_done"], 1)
                    store_sums(act, L0, 0, l0_sums, 2 * i + s, s)
            act.wait_ge(L0["scale_ready"], 1)
            act.activation(l0_common[:, 2:3], l0_common[:, 1:2], ACT.Exp).then_inc(L0["exp_done"], 1)
            act.wait_ge(L0["scale_ready"], 2)
            act.activation(diag[:, 3, :], diag[:, 2, :], ACT.Exp).then_inc(L0["exp_done"], 1)
            with act.Fori(0, LSTEPS) as i:
                std(1, i)
            act.wait_ge(S["zero_ready"], 2)
            fill2_rows = fill2.rearrange("(p k) w -> p (k w)", k=C)
            for n in range(2):
                act.dma_start(fill2_rows[:, n * ZCH:(n + 1) * ZCH], l1_zero).then_inc(L1["target_zeroed"], 16)
            with act.Fori(2, NB) as n:
                act.wait_ge(L1["sums_ready"], n - 1)
                act.dma_start(fill2_rows[:, bass.ds(n * ZCH, ZCH)], l1_zero).then_inc(L1["target_zeroed"], 16)
            def normed(i):
                std(2, i)
                act.wait_ge(S["x_ready"], NORMS[2] + 1 + i)

            linear_act(0, normed)
            act.wait_ge(L2["diff_ready"], 1)
            act.activation(l2_logit, l2_m, ACT.Exp).then_inc(L2["exp_ready"], 1)
            def exponentials(b, r, i):
                act.wait_ge(L2["scaled"], b * 2 + 2)
                act.activation(l2_z[r], l2_z[r], ACT.Exp).then_inc(L2["exp_done"], 1)

            def turn_sums(b, r, i):
                q = r % 2
                act.activation(l2_goes_on[q], bc(l2_cont[:, bass.ds(b * T, T)], [P, F, T], 1), ACT.Copy)\
                   .then_inc(L2["goes_on_ready"], 1)
                act.wait_ge(L2["msg_free"], b + 3)
                act.wait_ge(L2["stored"][q], i * (8 * ZRING) + r // 2 * 16)
                act.activation(l2_sums[q], l2_scanned[q].rearrange("p f t -> p t f"), ACT.Copy).then_inc(L2["sums_ready"], 1)

            z_blocks(act.Fori, 2, exponentials, turn_sums)
            linear_act(LSTEPS, lambda i: act.wait_ge(L2["inputs_ready"], i + 1), lambda i: std(3, i))
            act.wait_ge(S["x_ready"], NORMS[3] + LSTEPS)
            linear_act(2 * LSTEPS)
            with act.Fori(0, NPAIR) as i:
                for n in range(2 * NG):
                    q, turn = n % 2, i * NG + n // 2
                    act.wait_ge(L3["h_done"][q], turn + 1)
                    act.wait_ge(L3["w_done"][q], turn)
                    act.activation(l3_h[q][0:MLP, :], bank[q][0:MLP, 0, :], ACT.Relu, bias=w_mlp1[0:MLP, MLP:MLP + 1])\
                       .then_inc(L3["h_taken"][q], 1)

        @block.tensor
        def _(pe):
            pe.wait_ge(S["diag_ready"], 1)
            pe.matmul(bank[1][:, 0, 0:P], ones[:, :], diag[:, 0, :], start=True, stop=True).then_inc(S["rows_ready"], 1)
            pe.wait_ge(S["diag_ready"], 2)
            pe.matmul(bank[1][:, 1, 0:1], ones[:, :], unsorted_f[:, 0:1], start=True, stop=True).then_inc(S["rows_ready"], 1)
            pe.matmul(bank[0][:, 0, 0:J], zero_b, zero_b[:, 0:J], start=True, stop=False)
            with pe.Fori(0, C // (2 * KB)) as i:
                for s in range(2):
                    pe.wait_ge(S[f"onehot_made{s}"], i + 1)
                    for k in range(KB):
                        last = pe.matmul(bank[0][:, 0, 0:J], onehot_lo[s][:, k, :], onehot_hi[s][:, k, :],
                                         start=False, stop=False)
                    last.then_inc(S[f"onehot_used{s}"], 1)
            pe.matmul(bank[0][:, 0, 0:J], zero_b, zero_b[:, 0:J], start=False, stop=True).then_inc(S["hist_done"], 1)
            pe.wait_ge(S["cnt_ready"], 1)
            pe.matmul(bank[1][:, 0, 0:J], upto[:, :], stat[:, 0, :], start=True, stop=True)
            pe.matmul(bank[2][:, 0, 0:J], ones[:, :], stat[:, 0, :], start=True, stop=True).then_inc(S["prefix_done"], 1)
            is_unsorted = know_order(pe)
            with pe.If(is_unsorted != 0):
                with pe.Fori(0, C) as k:
                    pe.wait_ge(SORT["targets_ready"], k + 1)
                    pe.matmul(bank[2][:, 0, 0:P], ones[:, :], diag[:, 0, :], start=True, stop=True).then_inc(SORT["row_ready"], 1)
                with pe.Fori(0, C) as k:
                    pe.wait_ge(SORT["moved2"], k * 32 + 32)
                    pe.wait_ge(SORT["ef_ready"], k)
                    pe.transpose(bank[2][0:F, 0, 0:P], moved_ef, ident[:, :]).then_inc(SORT["ef_turned"], 1)
            pe.wait_ge(S["diag_ready"], 3)
            for c in range(2):
                last = pe.matmul(bank[1][:, 0, c * P:(c + 1) * P], ones[:, :], diag[:, c, :], start=True, stop=True)
            last.then_inc(S["rows_ready"], 1)
            pe.wait_ge(L0["last_ready"], 1)
            pe.matmul(bank[1][:, 0, 0:P], ones[:, :], diag[:, 0, :], start=True, stop=True).then_inc(L0["max_rows_ready"], 1)
            pe.wait_ge(L0["last_ready"], 2)
            pe.matmul(bank[2][:, 0, 0:P], ones[:, :], diag[:, 1, :], start=True, stop=True).then_inc(L0["max_rows_ready"], 1)
            pe.wait_ge(L0["last_ready"], 3)
            pe.matmul(bank[3][:, 0, 0:F + 1], diag[:, 3, :], l0_last[:, 0:F + 1], start=True, stop=True)\
              .then_inc(S["carry_done"], 1)

            def carry(done, count, last_sums):
                pe.wait_ge(done, count)
                pe.matmul(bank[3][:, 0, 0:F], from_left[:, :], last_sums, start=True, stop=True).then_inc(S["carry_done"], 1)

            def linear_pe(cols, depth, turns):
                m = cols.shape[1]
                with pe.Fori(0, LSTEPS) as i:
                    for s in range(2):
                        pe.wait_ge(LIN["staged"][s], i + turns + 1)
                        pe.wait_ge(LIN["t_ready"][s], i + turns)
                        for j in range(LT):
                            last = pe.transpose(flat(bank[s])[0:F, j * P:(j + 1) * P], lin_in[s][:, j, :], ident[:, :])
                        last.then_inc(LIN["transposed"][s], 1)
                    for s in range(2):
                        pe.wait_ge(LIN["t_ready"][s], i + turns + 1)
                        pe.wait_ge(LIN["taken"][s], i + turns)
                        for j in range(LT):
                            last = pe.matmul(flat(bank[2 + s])[:, j * m:(j + 1) * m], lin_t[s][0:depth, j * P:(j + 1) * P],
                                             cols, start=True, stop=True)
                        last.then_inc(LIN["done"][s], 1)

            carry(L1["rows_free"], NB + 2, l1_carry)
            pe.wait_ge(S["w_loaded"], 16 * 11)
            pe.wait_ge(L2["ones_ready"], 2)
            linear_pe(w_node[0:F + 1, 0:P], F + 1, 0)
            for n in range(4):
                pe.wait_ge(L2["diags_ready"], n + 1)
                pe.matmul(bank[n][:, 0, 0:P], ones[:, :], diag[:, n, :], start=True, stop=True).then_inc(L2["rows_ready"], 1)
            pe.wait_ge(L2["ends_ready"], 1)
            pe.matmul(bank[0][:, 1, 0:2], from_left[:, :], ends[:, 0:2], start=True, stop=True)
            pe.matmul(bank[1][:, 1, 0:2], from_right[:, :], ends[:, 2:4], start=True, stop=True).then_inc(L2["others_ready"], 1)
            carry(L2["msg_free"], NB + 2, l2_scanned[1][:, :, T - 1])
            linear_pe(w_node[0:F + 1, P:P + F], F + 1, LSTEPS)
            pe.wait_ge(L3["ones_ready"], 4)
            linear_pe(w_node[0:F, P + F:P + 2 * F], F, 2 * LSTEPS)
            for s in range(2):
                pe.wait_ge(LIN["taken"][s], 3 * LSTEPS)
            with pe.Fori(0, NPAIR) as i:
                def hidden(n):
                    q, turn = n % 2, i * NG + n // 2
                    s, g = divmod(n, NG)
                    if g == 0:
                        pe.wait_ge(L3["mlp_loaded"][s], i * 16 + 16)
                    pe.wait_ge(L3["h_taken"][q], turn)
                    pe.matmul(bank[q][0:MLP, 0, :], w_mlp1[0:F, 0:MLP], l3_ef[s][:, g * GT * P:(g + 1) * GT * P],
                              start=True, stop=True).then_inc(L3["h_done"][q], 1)

                hidden(0)
                for n in range(2 * NG):
                    q, turn = n % 2, i * NG + n // 2
                    if n + 1 < 2 * NG:
                        hidden(n + 1)
                    pe.wait_ge(L3["h_taken"][q], turn + 1)
                    pe.wait_ge(L3["w_taken"][q], turn)
                    for t in range(GT):
                        last = pe.matmul(flat(bank[2 + q])[:, t * WN:(t + 1) * WN], l3_h[q][:, t * P:(t + 1) * P],
                                         w_mlp2[:, :], start=True, stop=True)
                    last.then_inc(L3["w_done"][q], 1)
            carry(L3["carry_ready"], NB + 1, l3_carry)

        @block.vector
        def _(v):
            dve = Steps(v, step)
            run = dve.then_wait

            def layer_norm(n, i, x, centred, sq, h):
                count = x.shape[1]
                mean, var, std, scale = (stat[:, k, 0:count] for k in range(4))
                run(v.tensor_reduce(mean, x, AX.X, ALU.add))
                run(v.tensor_scalar(mean, mean, 1.0 / F, None, ALU.mult))
                run(v.tensor_tensor(centred, x, bc(mean, [P, count, F], 2), ALU.subtract))
                run(v.tensor_tensor(sq, centred, centred, ALU.mult))
                run(v.tensor_reduce(var, sq, AX.X, ALU.add))
                v.tensor_scalar(var, var, 1.0 / F, EPS, ALU.mult, ALU.add).then_inc(S["var_ready"], 1)
                v.wait_ge(S["std_ready"], NORMS[n] + 1 + i)
                run(v.reciprocal(scale, std))
                v.scalar_tensor_tensor(h, centred, 0.0, bc(scale, [P, count, F], 2), ALU.max, ALU.mult)\
                 .then_inc(S["x_ready"], 1)
                v.wait_ge(S["x_ready"], NORMS[n] + 1 + i)

            def norm_chunk(n, i):
                js = bass.ds(i * CHUNK, CHUNK)
                v.tensor_scalar(x_sb[:, js, :], chunk_x, 1.0, None, ALU.mult).then_inc(S["x_updated"], 1)
                layer_norm(n, i, chunk_x, chunk_h, chunk_sq, h_sb[:, js, :])
                v.wait_ge(S["x_updated"], NORMS[n] + i)

            def start_blocks(L, carry):
                v.memset(carry, 0.0).then_inc(L["rows_free"], 2)

            def scan_block(L, rows, to, carry, b, turn, s):
                v.wait_ge(L["stored"][s], turn * 16)
                v.wait_ge(L["rows_free"], b + 2)
                for f in range(F):
                    ins = v.tensor_tensor_scan(to[:, :, f], cont[:, bass.ds(b * T, T)], rows[:, :, f], carry[:, f:f + 1],
                                               ALU.mult, ALU.add)
                ins.then_inc(L["sums_ready"], 1)
                v.wait_ge(L["sums_ready"], b + 1)
                v.tensor_copy(carry, to[:, T - 1, :]).then_inc(L["rows_free"], 1)

            def fix_sums(n):
                v.wait_ge(S["carry_done"], n + 1)
                v.wait_ge(S["fix_fetched"], 16 * (n + 1))
                v.tensor_tensor(row_fix[:, 0:F], row_fix[:, 0:F], bank[3][:, 0, 0:F], ALU.add).then_inc(S["fix_ready"], 1)
                v.wait_ge(S["fix_scattered"], 16 * (n + 1))

            def node_sums(n, i, width=F):
                js = bass.ds(i * CHUNK, CHUNK)
                y = fetched[:, 0:J * width].rearrange("p (j w) -> p j w", w=width)[:, js, 0:F]
                for s in range(2):
                    v.wait_ge(S[f"nodes_fetched{s}"], i * (16 * LT) + 16 * LT * (n * LSTEPS + 1))
                if n:
                    run(v.tensor_tensor(y, y, bc(has_edges[:, js], [P, CHUNK, F], 2), ALU.mult))
                return y, js

            def linear_add(turns, i, to_chunk=None):
                for s in range(2):
                    v.wait_ge(LIN["done"][s], i + turns + 1)
                    got = flat(bank[2 + s])[:, 0:LT * F].rearrange("p (j f) -> p j f", f=F)
                    x = x_sb[:, bass.ds((2 * i + s) * LT, LT), :]
                    to = to_chunk[:, s * LT:(s + 1) * LT, :] if to_chunk is not None else x
                    v.tensor_tensor(to, x, got, ALU.add).then_inc(LIN["taken"][s], 1)

            v.memset(l0_zero, 0.0).then_inc(S["zero_ready"], 1)
            run(v.memset(ones[:, :], 1.0))
            run(v.memset(zero_b, 0.0))
            v.wait_ge(S["iota_made"], 3)
            run(v.tensor_copy(iota_f[:, :], iota_i[:, :]))
            run(v.tensor_copy(iota_b[:, :], iota_i[:, :]))
            v.tensor_copy(part_f[:, :], part_i[:, :]).then_inc(L0["rows_free"], RING)
            v.wait_ge(L0["rows_free"], RING)
            for to, op in ((ident, ALU.is_equal), (before, ALU.is_gt), (after, ALU.is_lt), (upto, ALU.is_ge)):
                run(v.tensor_scalar(to[:, :], iota_f[:, :], part_f[:, 0:1], None, op))
            v.wait_ge(S["dst_loaded"], 16)
            run(v.tensor_copy(dst_f, dst_i))
            v.tensor_scalar(diag[:, 0, :], ident[:, :], dst_f[:, 0:1], None, ALU.mult).then_inc(S["diag_ready"], 1)
            run(v.tensor_tensor(h_flat[:, 0:C - 1], dst_f[:, 0:C - 1], dst_f[:, 1:C], ALU.is_gt))
            run(v.tensor_reduce(unsorted_f[:, 0:1], h_flat[:, 0:C - 1], AX.X, ALU.add))
            v.wait_ge(S["rows_ready"], 1)
            run(v.scalar_tensor_tensor(diag[:, 1, :], bank[1][:, 0, 0:P], dst_f[:, C - 1:C], before[:, :],
                                       ALU.is_lt, ALU.mult))
            run(v.tensor_reduce(unsorted_f[:, 1:2], diag[:, 1, :], AX.X, ALU.add))
            v.tensor_tensor(unsorted_f[:, 0:1], unsorted_f[:, 0:1], unsorted_f[:, 1:2], ALU.add).then_inc(S["diag_ready"], 1)
            v.wait_ge(S["rows_ready"], 2)
            v.tensor_scalar(unsorted_i[:, :], bank[1][:, 1, 0:1], 0.0, None, ALU.is_gt).then_inc(S["order_known"], 1)
            v.wait_ge(S["x_loaded"], 16)
            prod = fetched[:, 0:J * F].rearrange("p (j f) -> p j f", f=F)
            layer_norm(0, 0, x_sb[:, :, :], h_sb[:, :, :], prod, h_sb[:, :, :])
            v.wait_ge(S["attn_loaded"], 32)
            run(v.tensor_tensor(prod, h_sb[:, :, :], bc(attn_bc[:, 0, 0:F], [P, J, F], 1), ALU.mult))
            run(v.tensor_reduce(l0_table[:, :, F], prod, AX.X, ALU.add))
            run(v.tensor_tensor(prod, h_sb[:, :, :], bc(attn_bc[:, 0, F:2 * F], [P, J, F], 1), ALU.mult))
            v.tensor_reduce(l0_table[:, :, F + 1], prod, AX.X, ALU.add).then_inc(S["table_ready"], 1)
            v.wait_ge(S["table_ready"], 2)
            bits = h_flat.bitcast(I32)
            run(v.tensor_scalar(bits, dst_i, P - 1, None, ALU.bitwise_and))
            v.tensor_copy(dst_lo, bits).then_inc(S["onehot_used0"], 1)
            v.wait_ge(S["onehot_used0"], 1)
            run(v.tensor_scalar(bits, dst_i, P.bit_length() - 1, None, ALU.logical_shift_right))
            v.tensor_copy(dst_hi, bits).then_inc(S["onehot_used1"], 1)
            v.wait_ge(S["onehot_used1"], 1)
            with v.Fori(0, C // (2 * KB)) as i:
                for s in range(2):
                    v.wait_ge(S[f"onehot_used{s}"], i + 1)
                    at_k = i * (2 * KB) + s * KB
                    v.tensor_tensor(onehot_lo[s], bc(dst_lo[:, bass.ds(at_k, KB)], [P, KB, P], 2),
                                    bc(iota_b[:, :], [P, KB, P], 1), ALU.is_equal)
                    v.tensor_tensor(onehot_hi[s], bc(dst_hi[:, bass.ds(at_k, KB)], [P, KB, J], 2),
                                    bc(iota_b[:, 0:J], [P, KB, J], 1), ALU.is_equal).then_inc(S[f"onehot_made{s}"], 1)
            v.wait_ge(S["hist_done"], 1)
            v.tensor_copy(stat[:, 0, :], bank[0][:, 0, 0:J]).then_inc(S["cnt_ready"], 1)
            v.wait_ge(S["prefix_done"], 1)
            v.wait_ge(S["cnt_ready"], 1)
            run(v.tensor_tensor_scan(stat[:, 1, :], ones[:, 0:J], bank[2][:, 0, 0:J], 0.0, ALU.mult, ALU.add))
            run(v.tensor_tensor(stat[:, 1, :], stat[:, 1, :], bank[2][:, 0, 0:J], ALU.subtract))
            run(v.tensor_tensor(stat[:, 1, :], stat[:, 1, :], bank[1][:, 0, 0:J], ALU.add))
            run(v.tensor_tensor(stat[:, 2, :], stat[:, 1, :], stat[:, 0, :], ALU.subtract))
            run(v.tensor_scalar(stat[:, 1, :], stat[:, 1, :], 1.0, 0.0, ALU.subtract, ALU.max))
            run(v.tensor_scalar(stat[:, 3, :], stat[:, 0, :], 0.0, float(EP), ALU.is_equal, ALU.mult))
            run(v.tensor_tensor(stat[:, 2, :], stat[:, 2, :], stat[:, 3, :], ALU.add))
            run(v.tensor_copy(node_idx[:, 0, :], stat[:, 1, :]))
            run(v.tensor_copy(node_idx[:, 1, :], stat[:, 2, :]))
            run(v.tensor_copy(node_idx[:, 2, :], stat[:, 0, :]))
            is_unsorted = know_order(v)
            v.tensor_scalar(unsorted_f[:, 1:2], unsorted_f[:, 0:1], 1.0, None, ALU.mult).then_inc(S["node_idx_ready"], 1)
            with v.If(is_unsorted != 0):
                sort = Steps(v, SORT["dve_step"])
                then = sort.then_wait
                target, rank, total, cursor, edge, last, nowhere = (col_f[:, n:n + 1] for n in range(7))
                then(v.tensor_scalar(edge, part_f[:, 1:2], 1.0, None, ALU.subtract))
                with sort.loop(C, 14) as k:
                    v.wait_ge(SORT["placed"], k * 32)
                    then(v.tensor_scalar(col_i[:, 0:1], dst_i[:, bass.ds(k, 1)], 1.0, None, ALU.mult))
                    then(v.tensor_copy(target, col_i[:, 0:1]))
                    v.tensor_scalar(diag[:, 0, :], ident[:, :], target, None, ALU.mult).then_inc(SORT["targets_ready"], 1)
                    then(v.tensor_scalar(edge, edge, 1.0, None, ALU.add))
                    then(v.tensor_copy(col_i[:, 1:2], edge))
                    v.wait_ge(SORT["row_ready"], k + 1)
                    then(v.tensor_scalar(same, bank[2][:, 0, 0:P], target, None, ALU.is_equal))
                    then(v.tensor_tensor(same_low, same, after[:, :], ALU.mult))
                    then(v.tensor_reduce(rank, same_low, AX.X, ALU.add))
                    then(v.tensor_reduce(total, same, AX.X, ALU.add))
                    then(v.tensor_scalar(last, rank, 1.0, total, ALU.add, ALU.is_equal))
                    then(v.tensor_scalar(nowhere, last, 1.0, -float(NP), ALU.subtract, ALU.mult))
                    then(v.tensor_tensor(col_i[:, 3:4], target, nowhere, ALU.add))
                    v.wait_ge(SORT["cursor_fetched"], k * 16 + 16)
                    then(v.tensor_copy(cursor, cursor_i))
                    then(v.tensor_tensor(col_i[:, 2:3], cursor, rank, ALU.add))
                    then(v.tensor_tensor(cursor, cursor, total, ALU.add))
                    v.tensor_copy(cursor_i, cursor).then_inc(SORT["place_ready"], 1)
                v.wait_ge(SORT["order_loaded"], 16)
                with v.Fori(0, C) as k:
                    wait_moved(v, k)
                    v.tensor_scalar(order_col, order_i[:, bass.ds(k, 1)], 1.0, None, ALU.mult)\
                     .then_inc(SORT["column_ready"], 1)
            v.wait_ge(S["dst_loaded"], 48)
            run(v.tensor_copy(dst_f, dst_i))
            run(v.tensor_copy(dst_ends[:, 0:1], dst_f[:, 0:1]))
            run(v.tensor_copy(dst_ends[:, 1:2], dst_f[:, C - 1:C]))
            run(v.memset(cont[:, :], 0.0))
            run(v.tensor_tensor(cont[:, 1:C], dst_f[:, 1:C], dst_f[:, 0:C - 1], ALU.is_equal))
            run(v.tensor_scalar(cont_big[:, :], cont[:, :], 1.0, BIG, ALU.subtract, ALU.mult))
            run(v.tensor_scalar(h_flat, dst_f, dst_ends[:, 0:1], None, ALU.is_equal))
            run(v.tensor_reduce(first_len[:, 0:1], h_flat, AX.X, ALU.add))
            run(v.tensor_scalar(first_len[:, 1:2], first_len[:, 0:1], part_f[:, 1:2], 1.0, ALU.add, ALU.subtract))
            run(v.tensor_copy(first_end_i[:, :], first_len[:, 1:2]))
            run(v.tensor_scalar(diag[:, 0, :], ident[:, :], dst_ends[:, 0:1], None, ALU.mult))
            v.tensor_scalar(diag[:, 1, :], ident[:, :], dst_ends[:, 1:2], None, ALU.mult).then_inc(S["diag_ready"], 1)
            v.wait_ge(S["rows_ready"], 3)
            run(v.scalar_tensor_tensor(from_left[:, :], bank[1][:, 0, 0:P], dst_ends[:, 1:2], before[:, :],
                                       ALU.is_equal, ALU.mult))
            run(v.scalar_tensor_tensor(from_right[:, :], bank[1][:, 0, P:2 * P], dst_ends[:, 0:1], after[:, :],
                                       ALU.is_equal, ALU.mult))
            v.wait_ge(S["node_idx_loaded"], 16)
            run(v.tensor_scalar(has_edges[:, :], node_idx[:, 2, :], 1.0, None, ALU.min))
            v.wait_ge(L0["target_loaded"], 16)
            v.wait_ge(L0["first_fetched"], 16)
            run(v.tensor_copy(l0_target[:, 0:1], row_fix[:, F + 1:F + 2]))
            run(v.tensor_tensor_scan(l0_target, cont[:, 0:C], l0_target, 0.0, ALU.mult, ALU.add))
            run(v.memset(l0_last, 0.0))
            run(v.memset(l0_max, 0.0))
            with dve.loop(NPAIR, 18) as i:
                for s in range(2):
                    b = i * 2 + s
                    k = b * T
                    rows = l0_rows((i % (RING // 2)) * (2 * T * W0) + s * T * W0)
                    v.wait_ge(L0["gathered"][s], i * (16 * T) + 16 * T)
                    run(v.tensor_tensor(l0_e, rows[:, :, F], l0_target[:, bass.ds(k, T)], ALU.add))
                    run(v.scalar_tensor_tensor(l0_e, l0_e, 0.01, l0_e, ALU.mult, ALU.max))
                    run(v.tensor_tensor_scan(l0_max[:, bass.ds(k + 1, T)], cont_big[:, bass.ds(k, T)], l0_e,
                                             l0_max[:, bass.ds(k, 1)], ALU.add, ALU.max))
                    run(v.tensor_tensor(l0_diff[:, 0, :], l0_max[:, bass.ds(k, T)], l0_max[:, bass.ds(k + 1, T)], ALU.subtract))
                    run(v.tensor_scalar(l0_diff[:, 0, :], l0_diff[:, 0, :], 0.0, None, ALU.min))
                    v.tensor_tensor(l0_diff[:, 1, :], l0_e, l0_max[:, bass.ds(k + 1, T)], ALU.subtract)\
                     .then_inc(L0["diff_ready"], 1)
                    v.wait_ge(L0["exp_done"], b + 1)
                    run(v.tensor_tensor(l0_exp[:, 0, :], l0_exp[:, 0, :], cont[:, bass.ds(k, T)], ALU.mult))
                    run(v.tensor_tensor(rows[:, :, 0:F], rows[:, :, 0:F], bc(l0_exp[:, 1, :], [P, T, F], 2), ALU.mult))
                    v.wait_ge(L0["stored"][s], i * 16)
                    for f in range(F + 1):
                        data = rows[:, :, f] if f < F else l0_exp[:, 1, :]
                        ins = v.tensor_tensor_scan(l0_sums[s][:, :, f], l0_exp[:, 0, :], data, l0_last[:, f:f + 1],
                                                   ALU.mult, ALU.add)
                    run(ins)
                    run(v.tensor_copy(l0_last[:, 0:F + 1], l0_sums[s][:, T - 1, 0:F + 1]))
                    v.tensor_scalar(l0_sums[s][:, :, F + 1], l0_max[:, bass.ds(k + 1, T)], 1.0, None, ALU.mult)\
                     .then_inc(L0["sums_ready"], 1)
                    v.tensor_scalar(l0_last[:, F + 1:F + 2], l0_max[:, bass.ds(k + T, 1)], 1.0, None, ALU.mult)\
                     .then_inc(L0["rows_free"], 1)
                    v.wait_ge(L0["rows_free"], b + RING + 1)
            v.tensor_scalar(diag[:, 0, :], ident[:, :], l0_last[:, F + 1:F + 2], None, ALU.mult).then_inc(L0["last_ready"], 1)
            v.wait_ge(L0["max_rows_ready"], 1)
            common, own_diff, own_weight = (l0_common[:, n:n + 1] for n in range(3))
            run(v.tensor_tensor(diag[:, 1, :], from_right[:, :], bank[1][:, 0, 0:P], ALU.mult))
            run(v.tensor_scalar(diag[:, 2, :], from_right[:, :], 1.0, BIG, ALU.subtract, ALU.mult))
            run(v.tensor_tensor(diag[:, 1, :], diag[:, 1, :], diag[:, 2, :], ALU.add))
            run(v.tensor_reduce(common, diag[:, 1, :], AX.X, ALU.max))
            v.wait_ge(S["fix_fetched"], 16)
            run(v.tensor_tensor(common, common, row_fix[:, F + 1:F + 2], ALU.max))
            v.tensor_tensor(own_diff, row_fix[:, F + 1:F + 2], common, ALU.subtract).then_inc(L0["scale_ready"], 1)
            v.tensor_scalar(diag[:, 1, :], ident[:, :], common, None, ALU.mult).then_inc(L0["last_ready"], 1)
            v.wait_ge(L0["max_rows_ready"], 2)
            run(v.tensor_scalar(diag[:, 2, :], bank[2][:, 0, 0:P], l0_last[:, F + 1:F + 2], -1.0, ALU.subtract, ALU.mult))
            v.tensor_scalar(diag[:, 2, :], diag[:, 2, :], 0.0, None, ALU.min).then_inc(L0["scale_ready"], 1)
            v.wait_ge(L0["exp_done"], NB + 2)
            v.tensor_tensor(diag[:, 3, :], diag[:, 3, :], from_left[:, :], ALU.mult).then_inc(L0["last_ready"], 1)
            v.wait_ge(S["carry_done"], 1)
            v.scalar_tensor_tensor(row_fix[:, 0:F + 1], row_fix[:, 0:F + 1], own_weight, bank[3][:, 0, 0:F + 1],
                                   ALU.mult, ALU.add).then_inc(S["fix_ready"], 1)
            v.wait_ge(S["fix_scattered"], 16)
            start_blocks(L1, l1_carry)
            v.memset(l1_zero, 0.0).then_inc(S["zero_ready"], 1)
            with dve.loop(LSTEPS, 10) as i:
                weight = stat[:, 0, 0:CHUNK]
                y, js = node_sums(0, i, W0)
                denominator = fetched[:, 0:J * W0].rearrange("p (j w) -> p j w", w=W0)[:, js, F]
                run(v.reciprocal(weight, denominator))
                run(v.tensor_tensor(weight, weight, has_edges[:, js], ALU.mult))
                run(v.tensor_tensor(y, y, bc(weight, [P, CHUNK, F], 2), ALU.mult))
                run(v.tensor_tensor(chunk_x, x_sb[:, js, :], y, ALU.add))
                norm_chunk(1, i)

            with dve.loop(NPAIR, 2) as i:
                for s in range(2):
                    v.wait_ge(L1["edge_loaded"][s], i * 16 + 16)
                    v.wait_ge(L1["gathered"][s], i * (16 * T) + 16 * T)
                    run(v.tensor_tensor(l1_rows[s], l1_rows[s], bc(l1_w[s], [P, T, F], 2), ALU.mult))
                    scan_block(L1, l1_rows[s], l1_sums[s], l1_carry, 2 * i + s, i, s)
            fix_sums(1)
            v.wait_ge(L1["target_zeroed"], 16 * NB)
            for s in range(2):
                v.memset(lin_t[s][F:F + 1, :], 1.0).then_inc(L2["ones_ready"], 1)
            start_blocks(L2, l2_target_carry)
            with dve.loop(LSTEPS, 8) as i:
                y, js = node_sums(1, i)
                run(v.tensor_tensor(chunk_x, x_sb[:, js, :], y, ALU.add))
                norm_chunk(2, i)
                for s in range(2):
                    v.wait_ge(LIN["done"][s], i + 1)
                    got = flat(bank[2 + s])[:, 0:LT * P].rearrange("p (j f) -> p j f", f=P)
                    v.tensor_scalar(l2_tabs[:, bass.ds((2 * i + s) * LT, LT), :], got, 1.0, None, ALU.mult)\
                     .then_inc(LIN["taken"][s], 1)
            with dve.loop(NPAIR, 12) as i:
                for s in range(2):
                    b = 2 * i + s
                    rows, edge = l2_rows[s], l2_edge[s]
                    v.wait_ge(L2["target_loaded"], b * 16 + 16)
                    for f in range(HF):
                        ins = v.tensor_tensor_scan(l2_target[:, :, f], cont[:, bass.ds(b * T, T)], l2_target[:, :, f],
                                                   l2_target_carry[:, f:f + 1], ALU.mult, ALU.add)
                    run(ins)
                    run(v.tensor_copy(l2_target_carry, l2_target[:, T - 1, :]))
                    v.wait_ge(L2["edge_loaded"][s], i * 16 + 16)
                    v.wait_ge(L2["gathered"][s], i * (16 * T) + 16 * T)
                    run(v.tensor_tensor(l2_target, l2_target, rows, ALU.add))
                    v.tensor_tensor(edge, edge, rows, ALU.mult).then_inc(L2["rows_free"], 1)
                    v.wait_ge(L2["rows_free"], b + 3)
                    run(v.scalar_tensor_tensor(l2_target, l2_target, 0.2, l2_target, ALU.mult, ALU.max))
                    by_head = edge.rearrange("p t (h f) -> p t h f", h=2)
                    run(v.tensor_reduce(l2_top, by_head, AX.X, ALU.max))
                    run(v.tensor_tensor(l2_target, l2_target, bc(attn_bc[:, 1, :], [P, T, HF], 1), ALU.mult))
                    v.tensor_tensor(by_head, by_head, l2_top.unsqueeze(3).to_broadcast([P, T, 2, F]), ALU.subtract)\
                     .then_inc(L2["logits_ready"], 1)
                    v.tensor_reduce(l2_logit[:, :, bass.ds(b * T, T)].rearrange("p h t -> p t h"),
                                    l2_target.rearrange("p t (h f) -> p t h f", h=2), AX.X, ALU.add)\
                     .then_inc(L2["target_used"], 1)
                    v.wait_ge(L2["logits_ready"], b + 1)
                    v.wait_ge(L2["target_used"], b + 1)
            for s in range(2):
                v.wait_ge(L2["logits_stored"][s], 16 * NPAIR)
            for h in range(2):
                v.tensor_tensor_scan(l2_fwd[:, h, :], cont_big[:, 0:C], l2_logit[:, h, :], -BIG, ALU.add, ALU.max)
                ins = v.tensor_tensor_scan(l2_bwd[:, h, ::-1], cont_big[:, C:0:-1], l2_logit[:, h, ::-1], -BIG,
                                           ALU.add, ALU.max)
            run(ins)
            for n in range(4):
                end = l2_fwd[:, n, C - 1:C] if n < 2 else l2_bwd[:, n - 2, 0:1]
                v.tensor_scalar(diag[:, n, :], ident[:, :], end, None, ALU.mult).then_inc(L2["diags_ready"], 1)
            v.wait_ge(L2["dst_loaded"], 16)
            run(v.tensor_copy(l2_mask[:, 0, :], l2_dst_i))
            for n in range(2):
                run(v.tensor_scalar(l2_mask[:, 2 + n, :], l2_mask[:, 0, :], dst_ends[:, n:n + 1], None, ALU.is_equal))
            for n in range(2):
                ins = v.tensor_scalar(l2_mask[:, n, :], l2_mask[:, 2 + n, :], 1.0, BIG, ALU.subtract, ALU.mult)
            run(ins)
            run(v.tensor_tensor(l2_m, l2_fwd, l2_bwd, ALU.max))
            for n in range(4):
                which = from_right if n < 2 else from_left
                v.wait_ge(L2["rows_ready"], n + 1)
                run(v.tensor_scalar(l2_pick, which[:, :], 1.0, BIG, ALU.subtract, ALU.mult))
                run(v.tensor_tensor(diag[:, n, :], which[:, :], bank[n][:, 0, 0:P], ALU.mult))
                run(v.tensor_tensor(diag[:, n, :], diag[:, n, :], l2_pick, ALU.add))
                run(v.tensor_reduce(ends[:, 4 + n:5 + n], diag[:, n, :], AX.X, ALU.max))
            for n in range(4):
                h = n % 2
                run(v.scalar_tensor_tensor(l2_m[:, h, :], l2_mask[:, n // 2, :], ends[:, 4 + n:5 + n], l2_m[:, h, :],
                                           ALU.add, ALU.max))
            v.tensor_tensor(l2_m, l2_logit, l2_m, ALU.subtract).then_inc(L2["diff_ready"], 1)
            v.wait_ge(L2["exp_ready"], 1)
            for h in range(2):
                v.tensor_tensor_scan(l2_fwd[:, h, :], cont[:, 0:C], l2_logit[:, h, :], 0.0, ALU.mult, ALU.add)
                ins = v.tensor_tensor_scan(l2_bwd[:, h, ::-1], cont[:, C:0:-1], l2_logit[:, h, ::-1], 0.0, ALU.mult, ALU.add)
            run(ins)
            for n in range(4):
                end = l2_fwd[:, n, C - 1:C] if n < 2 else l2_bwd[:, n - 2, 0:1]
                ins = v.tensor_copy(ends[:, n:n + 1], end)
            ins.then_inc(L2["ends_ready"], 1)
            run(v.tensor_tensor(l2_m, l2_fwd, l2_bwd, ALU.add))
            run(v.tensor_tensor(l2_m, l2_m, l2_logit, ALU.subtract))
            v.wait_ge(L2["others_ready"], 1)
            for n in range(4):
                h = n % 2
                run(v.scalar_tensor_tensor(l2_m[:, h, :], l2_mask[:, 2 + n // 2, :], bank[n // 2][:, 1, h:h + 1],
                                           l2_m[:, h, :], ALU.mult, ALU.add))
            v.tensor_scalar(l2_m, l2_m, 1e-9, None, ALU.max).then_inc(L2["alpha_ready"], 1)
            v.wait_ge(L2["alpha_ready"], 1)
            run(v.tensor_copy(l2_cont, cont[:, 0:C]))
            run(v.memset(l2_cont[:, ::T], 0.0))
            v.memset(l2_scanned[1], 0.0).then_inc(L2["msg_free"], 2)
            with dve.loop(NB // ZRING, 1) as i:
                turn = bass.ds(i * (ZRING * T), ZRING * T)
                run(v.reciprocal(l2_m[:, :, turn], l2_m[:, :, turn]))
                v.tensor_tensor(l2_logit[:, :, turn], l2_logit[:, :, turn], l2_m[:, :, turn], ALU.mult)\
                 .then_inc(L2["alpha_ready"], 1)
            def normalise(b, r, i):
                z, norm = l2_z[r].rearrange("p t (h f) -> p t h f", h=2), l2_norm[r % 2]
                v.wait_ge(L2["exp_done"], b + 1)
                run(v.tensor_reduce(norm, z, AX.X, ALU.add))
                run(v.reciprocal(norm, norm))
                v.tensor_tensor(z, z, norm.unsqueeze(3).to_broadcast([P, T, 2, F]), ALU.mult).then_inc(L2["normed"], 1)

            def scan_messages(b, r, i):
                q = r % 2
                v.wait_ge(L2["z_used"], b + 1)
                v.wait_ge(L2["msg_free"], b + 2)
                run(v.scalar_tensor_tensor(l2_msg[q][:, :, 0], l2_scanned[1 - q][:, :, T - 1], cont[:, bass.ds(b * T, 1)],
                                           l2_msg[q][:, :, 0], ALU.mult, ALU.add))
                v.wait_ge(L2["goes_on_ready"], b + 1)
                v.tensor_tensor_scan(flat(l2_scanned[q]), flat(l2_goes_on[q]), flat(l2_msg[q]), 0.0, ALU.mult, ALU.add)\
                 .then_inc(L2["msg_free"], 1)

            z_blocks(lambda start, stop: dve.loop(stop, 3 * ZRING), 1, normalise, scan_messages)
            fix_sums(2)
            def add_sums(i):
                y, js = node_sums(2, i)
                v.tensor_tensor(h_sb[:, js, :], h_sb[:, js, :], y, ALU.add).then_inc(L2["inputs_ready"], 1)

            def update_chunk(i):
                linear_add(LSTEPS, i, chunk_x)
                for s in range(2):
                    v.wait_ge(LIN["taken"][s], i + LSTEPS + 1)
                norm_chunk(3, i)

            add_sums(0)
            with dve.loop(LSTEPS - 1, 7) as i:
                add_sums(i + 1)
                update_chunk(i)
            update_chunk(LSTEPS - 1)

            start_blocks(L3, l3_carry)
            for q in range(2):
                v.memset(l3_h[q][MLP:MLP + 1, :], 1.0).then_inc(L3["ones_ready"], 1)
            v.wait_ge(S["w_loaded"], 16 * 11)
            v.tensor_scalar(w_node[0:F, P + F:P + 2 * F], w_node[0:F, P + F:P + 2 * F], MUL ** -0.5, None, ALU.mult)\
             .then_inc(L3["ones_ready"], 1)
            v.tensor_scalar(w_mlp2[:, :], w_mlp2[:, :], 0.25, None, ALU.mult).then_inc(L3["carry_ready"], 1)
            v.wait_ge(L3["carry_ready"], 1)
            dots = w_mlp2[:, 0:2 * MM].rearrange("p (o i) -> p o i", i=2 * MUL)[:, :, MUL:2 * MUL]
            v.tensor_scalar(dots, dots, 3.0 ** -0.5, None, ALU.mult).then_inc(L3["ones_ready"], 1)
            with v.Fori(0, LSTEPS) as i:
                linear_add(2 * LSTEPS, i)
            for s in range(2):
                v.wait_ge(LIN["taken"][s], 3 * LSTEPS)
            def scans(i, s, fs):
                if fs.start == 0:
                    v.wait_ge(L3["stored"][s], i * 16)
                    v.wait_ge(L3["carry_ready"], 2 * i + s + 1)
                for f in fs:
                    ins = v.tensor_tensor_scan(l3_sums[s][:, :, f], cont[:, bass.ds((2 * i + s) * T, T)], l3_msg[s][:, :, f],
                                               l3_carry[:, f:f + 1], ALU.mult, ALU.add)
                if fs.stop == F:
                    ins.then_inc(L3["sums_ready"], 1)
                    v.wait_ge(L3["sums_ready"], 2 * i + s + 1)
                    v.tensor_copy(l3_carry, l3_sums[s][:, T - 1, :]).then_inc(L3["carry_ready"], 1)

            def tensor_product(i, s, before=None):
                rows, sh = l3_rows[s], l3_sh[s]
                v.wait_ge(L3["products_ready"][s], i + 1)
                run(v.tensor_reduce(l3_scal[s][:, :, MUL:2 * MUL], l3_dot[s], AX.X, ALU.add))
                for g in range(NG):
                    n = s * NG + g
                    q, turn = n % 2, i * NG + n // 2
                    cols = slice(g * GT, (g + 1) * GT)
                    w = flat(bank[2 + q]).rearrange("p (t w) -> p t w", w=WN)
                    path = lambda k: w[:, :, k * MM:(k + 1) * MM].rearrange("p t (o i) -> p t o i", i=MUL)
                    v.wait_ge(L3["w_done"][q], turn + 1)
                    v.tensor_tensor(l3_p0.rearrange("p t (o i) -> p t o i", i=2 * MUL),
                                    w[:, :, 0:2 * MM].rearrange("p t (o i) -> p t o i", i=2 * MUL),
                                    bc(l3_scal[s][:, cols, :], [P, GT, MUL, 2 * MUL], 2), ALU.mult)
                    v.tensor_tensor(l3_p1[:, 0, :].rearrange("p (t o i) -> p t o i", o=MUL, i=MUL), path(2),
                                    bc(rows[:, cols, 0:MUL], [P, GT, MUL, MUL], 2), ALU.mult)
                    for m in range(3):
                        ins = v.tensor_tensor(l3_p1[:, 1 + m, :].rearrange("p (t o i) -> p t o i", o=MUL, i=MUL), path(3),
                                              bc(l3_vec[s][:, cols, m::3], [P, GT, MUL, MUL], 2), ALU.mult)
                    ins.then_inc(L3["w_taken"][q], 1)
                    if before and g * SCANS < F:
                        scans(*before, range(g * SCANS, min((g + 1) * SCANS, F)))
                    v.wait_ge(L3["w_taken"][q], turn + 1)
                    v.tensor_reduce(l3_msg[s][:, cols, 0:MUL], l3_p0.rearrange("p t (o i) -> p t o i", i=2 * MUL),
                                    AX.X, ALU.add)
                    run(v.tensor_reduce(l3_red[:, :, cols, :].rearrange("p k t o -> p k (t o)"),
                                        l3_p1.rearrange("p k (n i) -> p k n i", i=MUL), AX.X, ALU.add))
                vec = l3_msg[s][:, :, MUL:F].rearrange("p t (o m) -> p t o m", m=3)
                for m in range(3):
                    ins = v.tensor_tensor(vec[:, :, :, m], l3_red[:, 0, :, :],
                                          sh[:, :, 1 + m:2 + m].to_broadcast([P, T, MUL]), ALU.mult)
                run(ins)
                for m in range(3):
                    ins = v.tensor_tensor(vec[:, :, :, m], vec[:, :, :, m], l3_red[:, 1 + m, :, :], ALU.add)
                ins.then_inc(L3["rows_free"], 1)
                v.wait_ge(L3["rows_free"], 2 * i + s + 3)

            tensor_product(0, 0)
            with dve.loop(NPAIR - 1, 2 * (2 + NG)) as i:
                tensor_product(i, 1, (i, 0))
                tensor_product(i + 1, 0, (i, 1))
            tensor_product(NPAIR - 1, 1, (NPAIR - 1, 0))
            scans(NPAIR - 1, 1, range(F))
            fix_sums(3)
            with dve.loop(LSTEPS, 1) as i:
                y, js = node_sums(3, i)
                v.tensor_tensor(x_sb[:, js, :], x_sb[:, js, :], y, ALU.add).then_inc(S["x_updated"], 1)


def layout(inputs):
    import numpy as np

    def padded(name, rows, value=0):
        v = np.asarray(inputs[name])
        to = np.full((rows,) + v.shape[1:], value, v.dtype)
        to[:v.shape[0]] = v
        return to.reshape(rows, -1)

    def same(name):
        return np.ascontiguousarray(inputs[name])

    def by_output(w):
        w = w.reshape(-1, 4, MUL, MUL).transpose(0, 1, 3, 2)
        both = np.concatenate([w[:, 0], w[:, 3]], axis=2)
        return np.concatenate([v.reshape(len(w), -1) for v in (both, w[:, 1], w[:, 2])], axis=1)

    si = np.zeros((F, F), np.float32)
    si[:MUL, :MUL] = inputs["L3_gnn_si_w0"]
    for m in range(3):
        si[MUL + m::3, MUL + m::3] = inputs["L3_gnn_si_w1"]
    ef = padded("edge_attr_32", EP)
    return {
        "x": padded("x", NP),
        "src": padded("src", EP),
        "dst": padded("dst", EP, N_NODES),
        "edge_weight": padded("edge_weight", EP),
        "edge_attr4": padded("edge_attr_4", EP),
        "edge_attr3": padded("edge_attr3_2x32", EP),
        "ef": ef,
        "ef_t": np.ascontiguousarray(ef.reshape(P, C, F).transpose(2, 1, 0)).reshape(F, C * P),
        "attn0": same("L0_gnn_attn_w"),
        "attn2": same("L2_gnn_attn").reshape(HF),
        "W2s": same("L2_gnn_W2s"), "b2s": same("L2_gnn_b2s"),
        "W2d": same("L2_gnn_W2d"), "b2d": same("L2_gnn_b2d"),
        "W1": same("L2_gnn_W1"), "b1": same("L2_gnn_b1"),
        "si": si,
        "mlp_W1": same("L3_gnn_W1"), "mlp_b1": same("L3_gnn_b1"),
        "mlp_W2": np.ascontiguousarray(by_output(same("L3_gnn_W2"))),
        "mlp_b2": np.ascontiguousarray(by_output(same("L3_gnn_b2")[None])[0]),
    }


def kernel(**inputs):
    import concourse.bacc as bacc
    from concourse.bass_utils import run_bass_kernel_spmd

    arrays = layout(inputs)
    nc = bacc.Bacc("TRN2", target_bir_lowering=False, num_devices=1)
    aps = {n: nc.dram_tensor(f"in_{n}", v.shape, mybir.dt.from_np(v.dtype), kind="ExternalInput").ap()
           for n, v in arrays.items()}
    out = nc.dram_tensor("out_x", (NP, F), F32, kind="ExternalOutput").ap()
    build(nc, aps, out)
    r = run_bass_kernel_spmd(nc, [{f"in_{n}": v for n, v in arrays.items()}], core_ids=[0])
    return r.results[0]["out_x"][:N_NODES]
```
